# Optimizing a Trainium2 kernel written in Bass

```python
import numpy as np
import jax
import jax.numpy as jnp

def _softmax(x, axis=-1):
    return jax.nn.softmax(x, axis=axis)

def _gelu(x):
    return jax.nn.gelu(x, approximate=True)

def _silu(x):
    return jax.nn.silu(x)

def _sigmoid(x):
    return jax.nn.sigmoid(x)

def _layernorm(x, axis=-1, eps=1e-05):
    m = jnp.mean(x, axis=axis, keepdims=True)
    v = jnp.var(x, axis=axis, keepdims=True)
    return (x - m) / jnp.sqrt(v + eps)

def _scatter_add(tgt, idx, src, axis=0):
    return tgt.at[idx].add(src)

def _segment_sum(src, seg, n):
    return jax.ops.segment_sum(src, seg, n)
kernel_name = 'mk_adj_resnorm_d2_adj_r2_402dfb'

def setup_inputs(seed: int=0):
    np.random.seed(seed)
    _w = jnp.asarray

    def _rec_inputs():
        import jax
        import jax.numpy as jnp
        _gk = jax.random.key(seed)
        x = -0.0005207 + 1.001 * jax.random.normal(jax.random.fold_in(_gk, 1), (8192, 128), jnp.float32)
        _a = jax.random.bernoulli(jax.random.fold_in(_gk, 2), 0.000976562, (8192, 8192))
        _a = jnp.logical_or(_a, jnp.swapaxes(_a, -1, -2))
        _a = jnp.logical_or(_a, jnp.eye(8192, dtype=bool))
        _af = _a.astype(jnp.float32)
        _af = _af * jax.random.uniform(jax.random.fold_in(_gk, 3), (8192, 8192), jnp.float32, 0.05, 1)
        adj = _af
        return (x, adj)
    x, adj = _rec_inputs()

    def _L0_gnn_setup():
        import jax, jax.numpy as jnp
        import numpy as np
        N = 8192
        F_IN = 128
        F_OUT = 128
        key = jax.random.key(seed)
        k1, k2, k3, k4 = jax.random.split(key, 4)
        x = jax.random.normal(k1, (N, F_IN), dtype=jnp.float32)
        adj = jax.random.uniform(k2, (N, N), dtype=jnp.float32)
        bound = 1.0 / np.sqrt(2 * F_IN)
        W = jax.random.uniform(k3, (F_OUT, 2 * F_IN), minval=-bound, maxval=bound, dtype=jnp.float32)
        b = jax.random.uniform(k4, (F_OUT,), minval=-bound, maxval=bound, dtype=jnp.float32)
        return {'x': x, 'adj': adj, 'W': W, 'b': b}
    _L0_gnn_all = _L0_gnn_setup()
    _L0_gnn_in = {k: v for k, v in _L0_gnn_all.items() if k in ('W', 'b')}
    del _L0_gnn_all

    def _L1_gnn_setup():
        import jax, jax.numpy as jnp
        import numpy as np
        N = 4096
        IN_DIM = 128
        OUT_DIM = 128
        EDGE_P = 0.002
        key = jax.random.key(seed)
        k1, k2, k3, k4 = jax.random.split(key, 4)
        H = jax.random.normal(k1, (N, IN_DIM), dtype=jnp.float32)
        A = (jax.random.uniform(k2, (N, N)) < EDGE_P).astype(jnp.float32)
        limit = np.sqrt(6.0 / (IN_DIM + OUT_DIM)).astype(np.float32)
        W = jax.random.uniform(k3, (OUT_DIM, IN_DIM), minval=-limit, maxval=limit, dtype=jnp.float32)
        bound = 1.0 / np.sqrt(IN_DIM)
        b = jax.random.uniform(k4, (OUT_DIM,), minval=-bound, maxval=bound, dtype=jnp.float32)
        return {'H': H, 'A': A, 'W': W, 'b': b}
    _L1_gnn_all = _L1_gnn_setup()
    _L1_gnn_in = {k: v for k, v in _L1_gnn_all.items() if k in ('W', 'b')}
    del _L1_gnn_all
    return {'x': x, 'adj': adj, 'L0_gnn_W': _L0_gnn_in['W'], 'L0_gnn_b': _L0_gnn_in['b'], 'L1_gnn_W': _L1_gnn_in['W'], 'L1_gnn_b': _L1_gnn_in['b']}

def reference(x, adj, L0_gnn_W, L0_gnn_b, L1_gnn_W, L1_gnn_b):
    import jax
    import jax.numpy as jnp

    def _L0_gnn_ref(x, adj, W, b):
        import jax, jax.numpy as jnp
        import numpy as np
        N = 8192
        F_IN = 128
        F_OUT = 128
        neigh = adj @ x
        W_self = W[:, :F_IN]
        W_neigh = W[:, F_IN:]
        return x @ W_self.T + neigh @ W_neigh.T + b

    def _L1_gnn_ref(H, A, W, b):
        import jax, jax.numpy as jnp
        import numpy as np
        N = 4096
        IN_DIM = 128
        OUT_DIM = 128
        EDGE_P = 0.002
        n = A.shape[0]
        A_t = A + jnp.eye(n, dtype=A.dtype)
        D = A_t.sum(axis=1)
        D_inv = jnp.where(D > 0, D ** (-0.5), jnp.zeros_like(D))
        A_norm = D_inv[:, None] * A_t * D_inv[None, :]
        HW = H @ W.T + b
        return jax.nn.relu(A_norm @ HW)
    x = _layernorm(x + _L0_gnn_ref(x, adj, L0_gnn_W, L0_gnn_b), axis=-1)
    x = _layernorm(x + _L1_gnn_ref(x, adj, L1_gnn_W, L1_gnn_b), axis=-1)
    return x

_drawn_inputs = setup_inputs


def setup_inputs(seed=0):
    import zlib

    import numpy as np

    out = dict(_drawn_inputs(seed))
    spreads = {}
    factors = {}
    for name, (base, spread) in spreads.items():
        noise = np.random.default_rng([zlib.crc32(name.encode()), seed]).standard_normal(out[name].shape)
        drawn = base * np.exp(spread * noise) if base else spread * noise
        out[name] = jnp.asarray(drawn.astype(out[name].dtype))
    for name, factor in factors.items():
        out[name] = (out[name] * factor).astype(out[name].dtype)
    return out
```

```python
import concourse.bass as bass
from concourse import mybir
from contextlib import ExitStack, nullcontext

P = 128
F = 128
MB = 512
KC = MB // P
SB = 4
RAW = 4
HALF = KC // 2
RING = 4
EPS = 1e-5
TINY = 1.2e-38


def two_layers(nc, tiles, x_t, w0_t, w1_t, b0, b1, eye, out):
    fp32, fp32r = mybir.dt.float32, mybir.dt.float32r
    ALU, ACT = mybir.AluOpType, mybir.ActivationFunctionType
    N = x_t.shape[1]
    NB = N // MB
    NS = NB // SB
    HALVES = 2 * NB
    XLOADS = RAW
    XCOLS = N // XLOADS
    LAST = F - 1

    ROWS1 = [(0, 0, 1), (0, 1, SB), (1, 0, 1), (1, 1, SB)] + [(s, 0, SB) for s in range(2, NS)]
    ROWS2 = [(0, 0, 1), (0, 1, SB)] + [(s, 0, SB) for s in range(1, NS)]

    def pass2_tiles(s):
        return NB - SB * s

    def pass2_base(s):
        return NB * NB + sum(SB * pass2_tiles(t) for t in range(s))

    def span(eng, lo, hi):
        return nullcontext(lo) if hi - lo == 1 else eng.Fori(lo, hi)

    x1_spill = nc.dram_tensor("x1_spill", (NB, P, KC * F), fp32, kind="Internal").ap()
    low_spill = nc.dram_tensor("low_spill", (NB, P, MB), fp32, kind="Internal").ap()
    out_v = out.rearrange("(i c p) f -> i p c f", c=KC, p=P)

    ctx = ExitStack()
    with ctx:
        def sb(name, shape, dt=fp32):
            return ctx.enter_context(nc.sbuf_tensor(name, shape, dt))

        def pb(name):
            return ctx.enter_context(nc.psum_tensor(name, [P, MB], fp32))

        def sem(name):
            return ctx.enter_context(nc.semaphore(name))

        z_hi = sb("z_hi", [P, NB, KC, F], fp32r)
        z_lo = sb("z_lo", [P, NB, KC, F], fp32r)
        g_hi = sb("g_hi", [P, NB, KC, F], fp32r)
        g_lo = sb("g_lo", [P, NB, KC, F], fp32r)
        raw = sb("raw", [P, RAW, KC * MB])
        a_hi = sb("a_hi", [P, RING, HALF, MB], fp32r)
        a_lo = sb("a_lo", [P, RING, HALF, MB], fp32r)
        acc_t = sb("acc_t", [P, MB])
        feat = sb("feat", [P, KC * F])
        x1 = sb("x1", [P, KC, F])
        h = sb("h", [P, KC, F])
        wide = sb("wide", [P, KC * F])
        low = sb("low", [P, MB])
        ws_t = sb("ws_t", [P, F])
        w1_sb = sb("w1_sb", [P, F])
        ident = sb("ident", [P, P])
        ident_r = sb("ident_r", [P, P], fp32r)
        b1_bc = sb("b1_bc", [P, F])
        b0_col = sb("b0_col", [P, 1])
        b0_last = sb("b0_last", [P, 1])
        stats = sb("stats", [P, KC, 6])
        mean_var = sb("mean_var", [P, KC, 2])
        deg = sb("deg", [P, KC])
        deg_pos = sb("deg_pos", [P, KC])
        pow_in = sb("pow_in", [P, 2 * KC])
        pow_out = sb("pow_out", [P, 2 * KC])
        minus_half = sb("minus_half", [P, 2 * KC])
        dinv = sb("dinv", [P, NB * KC])

        wn_t = feat[:, 0:F]
        g_raw = wide[:, :].rearrange("p (c f) -> p c f", c=KC)
        relu_v = feat[:, :].rearrange("p (c f) -> p c f", c=KC)

        acc0 = pb("acc0")
        acc1 = pb("acc1")
        ps_tr = pb("ps_tr")
        ps_x1t = pb("ps_x1t")
        ps_hw = pb("ps_hw")
        ps_z = [pb(f"ps_z{n}") for n in range(2)]
        tr_v = ps_tr[:, :].rearrange("p (c f) -> p c f", c=KC)
        hw_v = ps_hw[:, :].rearrange("p (c f) -> p c f", c=KC)

        s_const = sem("const_loaded")
        s_b0 = sem("b0_loaded")
        s_fill = sem("constants_filled")
        s_idr = sem("ident_r_ready")
        s_w = sem("weights_shifted")
        s_raw = [sem(f"raw_loaded{n}") for n in range(RAW)]
        s_zp = sem("z_in_psum")
        s_zh = sem("z_hi_ready")
        s_z = sem("z_ready")
        s_hi = sem("a_hi_ready")
        s_lo = sem("a_lo_ready")
        s_used = sem("half_used")
        s_xt = sem("x_t_loaded")
        s_row = sem("layer0_row_done")
        s_ht = sem("h_t_ready")
        s_tr = sem("h_in_psum")
        s_hc = sem("h_copied")
        s_stat = sem("stats_ready")
        s_rstd = sem("rstd_ready")
        s_dinv = sem("dinv_ready")
        s_x1 = sem("x1_ready")
        s_x1st = sem("x1_stored")
        s_x1p = sem("x1_t_in_psum")
        s_x1t = sem("x1_t_ready")
        s_hw = sem("hw_in_psum")
        s_gr = sem("g_raw_ready")
        s_gh = sem("g_hi_ready")
        s_g = sem("g_ready")
        s_lowc = sem("low_copied")
        s_lowst = sem("low_stored")
        s_lowld = sem("low_loaded")
        s_oa = sem("first_half_copied")
        s_ot = sem("acc_t_ready")
        s_relu = sem("relu_ready")
        s_x1ld = sem("x1_loaded")
        s_y = sem("y_ready")
        s_x1free = sem("x1_free")
        s_lowfree = sem("low_free")
        s_yfree = sem("y_free")
        s_yst = sem("y_stored")
        s_dve = sem("dve_step")
        s_pool = sem("pool_step")
        s_apart = sem("wait_apart")

        block = ctx.enter_context(nc.Block())

        @block.sync
        def _(sp):
            sp.dma_start(ws_t[:, :], w0_t[0:F, :]).then_inc(s_const, 16)
            sp.dma_start(wn_t, w0_t[F:2 * F, :]).then_inc(s_const, 16)
            sp.dma_start(w1_sb[:, :], w1_t).then_inc(s_const, 16)
            sp.dma_start(ident[:, :], eye).then_inc(s_const, 16)
            sp.dma_start(b1_bc[:, :], b1.to_broadcast([P, F])).then_inc(s_const, 16)
            sp.dma_start(b0_col[:, :], b0).then_inc(s_const, 16)
            sp.dma_start(b0_last[:, :], b0[LAST:F, :].to_broadcast([P, 1])).then_inc(s_const, 16)
            for n in range(XLOADS):
                sp.dma_start(raw[:, n, 0:XCOLS], x_t[:, n * XCOLS:(n + 1) * XCOLS]).then_inc(s_raw[n], 16)

            def load(slot, tile):
                sp.dma_start(raw[:, slot, :],
                             tiles[bass.ds(tile, 1), :, :].rearrange("o p n -> p (o n)")
                             ).then_inc(s_raw[slot], 16)

            for n in range(RAW):
                sp.wait_ge(s_zp, (n + 1) * (NB // XLOADS))
                load(n, n)
            with sp.Fori(1, NB * NB // RAW) as quad:
                for n in range(RAW):
                    sp.wait_ge(s_lo, 2 * RAW * quad + 2 * (n - RAW) + 2)
                    load(n, quad * RAW + n)
            for s in range(NS):
                with sp.Fori(0, SB) as r:
                    with sp.Fori(0, pass2_tiles(s) // RAW) as quad:
                        done = pass2_base(s) + r * pass2_tiles(s) + quad * RAW
                        for n in range(RAW):
                            sp.wait_ge(s_lo, 2 * done + 2 * (n - RAW) + 2)
                            load(n, (SB * s + r) * NB + (NB - 1 - SB * s - n) - quad * RAW)

        @block.scalar
        def _(act):
            act.wait_ge(s_const, 7 * 16)
            act.sem_inc(s_relu, 1)
            nc.scalar.activation(ident_r[:, :], ident[:, :], ACT.Copy).then_inc(s_idr, 1)
            act.wait_ge(s_fill, 1)
            for j in range(NB):
                act.wait_ge(s_zp, j + 1)
                nc.scalar.activation(z_hi[:, j, :, 0:LAST],
                                     ps_z[j % 2][:, :].rearrange("p (c f) -> p c f", c=KC)[:, :, 0:LAST],
                                     ACT.Copy).then_inc(s_zh, 1)

            def split(done, t, hh):
                if hh == 0:
                    act.wait_ge(s_raw[t % RAW], (16 // RAW) * done + 16 * (t // RAW + 2))
                q = 2 * done + 2 * t + hh
                if not (isinstance(q, int) and q < RING):
                    act.wait_ge(s_used, q - RING + 1)
                n = (2 * t + hh) % RING
                nc.scalar.activation(a_hi[:, n, :, :],
                                     raw[:, t % RAW, hh * HALF * MB:(hh + 1) * HALF * MB]
                                     .rearrange("p (c m) -> p c m", c=HALF), ACT.Copy).then_inc(s_hi, 1)

            def evacuate_layer0(row):
                act.wait_ge(s_row, row + 1)
                nc.scalar.activation(acc_t[:, :], acc0[:, :], ACT.Identity, bias=b0_col[:, 0:1]
                                     ).then_inc(s_ht, 1)

            def evacuate_x1t(row):
                act.wait_ge(s_x1p, row + 1)
                nc.scalar.activation(feat[:, :], ps_x1t[:, :], ACT.Copy).then_inc(s_x1t, 1)

            def round_g(row):
                act.wait_ge(s_gr, row + 1)
                nc.scalar.activation(g_hi[:, bass.ds(row, 1), :, :].rearrange("p o c f -> p (o c) f"),
                                     g_raw, ACT.Copy).then_inc(s_gh, 1)

            def evacuate_low(row):
                act.wait_ge(s_used, HALVES * (row + 1))
                act.wait_ge(s_lowfree, row - SB + 1)
                nc.scalar.activation(low[:, :], acc1[:, :], ACT.Copy).then_inc(s_lowc, 1)

            def layer0_steps(q, with_low, row):
                if q == 2:
                    evacuate_layer0(row)
                if q == 3 and with_low:
                    evacuate_low(row)
                if q == 6:
                    evacuate_x1t(row)
                if q == 9:
                    round_g(row)

            for s, lo, hi in ROWS1:
                with span(act, lo, hi) as r:
                    row = SB * s + r
                    for q in range(HALVES):
                        split(row * NB, q // 2, q % 2)
                        if s + lo > 0:
                            layer0_steps(q, s * SB + lo > SB, row - 1)

            def copy_first(used, row):
                act.wait_ge(s_used, used)
                act.wait_ge(s_tr, NB + row)
                nc.scalar.activation(acc_t[:, :], acc0[:, :], ACT.Copy).then_inc(s_oa, 1)

            def relu(row):
                act.wait_ge(s_tr, NB + row + 1)
                act.wait_ge(s_stat, NB + row)
                for c in range(KC):
                    last = nc.scalar.activation(relu_v[:, c, :], tr_v[:, c, :], ACT.Relu,
                                                scale=dinv[:, bass.ds(row * KC + c, 1)])
                last.then_inc(s_relu, 1)

            for s, lo, hi in ROWS2:
                halves = 2 * pass2_tiles(s)
                with span(act, lo, hi) as r:
                    row = SB * s + r
                    done = pass2_base(s) + r * pass2_tiles(s)
                    for q in range(halves):
                        split(done, q // 2, q % 2)
                        if s + lo == 0:
                            layer0_steps(q, True, NB - 1)
                        elif q == 4:
                            relu(row - 1)
                        if s == 0 and q == halves // 2 + 2:
                            copy_first(2 * done + halves // 2, row)
            relu(NB - 1)

        @block.vector
        def _(dve):
            steps = [0]

            dve.wait_ge(s_const, 7 * 16)
            nc.vector.tensor_scalar(ws_t[:, 0:LAST], ws_t[:, 0:LAST], ws_t[:, LAST:F], None, ALU.subtract)
            nc.vector.tensor_scalar(wn_t[:, 0:LAST], wn_t[:, 0:LAST], wn_t[:, LAST:F], None, ALU.subtract)
            nc.vector.tensor_scalar(b0_col[:, :], b0_col[:, :], b0_last[:, 0:1], None, ALU.subtract
                                    ).then_inc(s_dve, 1)
            dve.wait_ge(s_dve, 1)
            nc.vector.tensor_tensor(b0_col[:, :], b0_col[:, :], ident[:, LAST:P], ALU.add)
            nc.vector.memset(ws_t[:, LAST:F], 0.0).then_inc(s_dve, 1)
            dve.wait_ge(s_dve, 2)
            nc.vector.tensor_tensor(ws_t[:, 0:LAST], ws_t[:, 0:LAST], ident[:, 0:LAST], ALU.add
                                    ).then_inc(s_dve, 1)
            dve.wait_ge(s_dve, 3)
            nc.vector.tensor_scalar(ws_t[:, 0:LAST], ws_t[:, 0:LAST], ident[:, LAST:P], None, ALU.subtract
                                    ).then_inc(s_w, 1)
            nc.vector.memset(z_hi[:, :, :, LAST:F].bitcast(fp32), 1.0)
            nc.vector.memset(z_lo[:, :, :, LAST:F].bitcast(fp32), 0.0)
            nc.vector.memset(h[:, :, LAST:F], 0.0)
            nc.vector.memset(minus_half[:, :], -0.5).then_inc(s_fill, 1)
            for j in range(NB):
                dve.wait_ge(s_zh, j + 1)
                nc.vector.tensor_tensor(z_lo[:, j, :, 0:LAST],
                                        ps_z[j % 2][:, :].rearrange("p (c f) -> p c f", c=KC)[:, :, 0:LAST],
                                        z_hi[:, j, :, 0:LAST].bitcast(fp32), ALU.subtract).then_inc(s_z, 1)

            def split(done, t, hh):
                dve.wait_ge(s_hi, 2 * done + 2 * t + hh + 1)
                n = (2 * t + hh) % RING
                nc.vector.tensor_tensor(a_lo[:, n, :, :],
                                        raw[:, t % RAW, hh * HALF * MB:(hh + 1) * HALF * MB]
                                        .rearrange("p (c m) -> p c m", c=HALF),
                                        a_hi[:, n, :, :].bitcast(fp32), ALU.subtract).then_inc(s_lo, 1)

            START = 3

            def statistics(before):
                dve.wait_ge(s_dve, before)
                for c in range(KC):
                    last = nc.vector.bn_stats(stats[:, c, :], h[:, c, :])
                last.then_inc(s_dve, 1)
                dve.wait_ge(s_dve, before + 1)
                dve.sem_inc(s_apart, 1)
                for c in range(KC):
                    last = nc.vector.bn_aggr(mean_var[:, c, :], stats[:, c, :])
                last.then_inc(s_stat, 1)

            def normalise(dst, signal, count):
                dve.wait_ge(s_rstd, count)
                for c in range(KC):
                    last = nc.vector.tensor_scalar(dst[:, c, :], h[:, c, :], mean_var[:, c, 0:1],
                                                   pow_out[:, c:c + 1], ALU.subtract, ALU.mult)
                last.then_inc(signal, 1)

            def norm_in(row):
                dve.wait_ge(s_tr, row + 1)
                dve.wait_ge(s_dinv, row + 1)
                nc.vector.tensor_copy(deg[:, :], tr_v[:, :, LAST])
                nc.vector.tensor_copy(h[:, :, 0:LAST], tr_v[:, :, 0:LAST]).then_inc(s_dve, 1)
                statistics(3 * row + START + 1)

            def norm_out(row):
                dve.wait_ge(s_x1free, row + 1)
                normalise(x1, s_x1, row + 1)

            def make_g(row):
                dve.wait_ge(s_hw, row + 1)
                nc.vector.tensor_tensor(g_raw, hw_v, b1_bc[:, :].unsqueeze(1).to_broadcast([P, KC, F]),
                                        ALU.add).then_inc(s_dve, 1)
                dve.wait_ge(s_dve, 3 * row + START + 3)
                dve.wait_ge(s_dinv, row + 2)
                nc.vector.tensor_tensor(g_raw, g_raw,
                                        dinv[:, bass.ds(row * KC, KC)].unsqueeze(2).to_broadcast([P, KC, F]),
                                        ALU.mult).then_inc(s_gr, 1)

            def split_g(row):
                dve.wait_ge(s_gh, row + 1)
                nc.vector.tensor_tensor(
                    g_lo[:, bass.ds(row, 1), :, :].rearrange("p o c f -> p (o c) f"), g_raw,
                    g_hi[:, bass.ds(row, 1), :, :].rearrange("p o c f -> p (o c) f").bitcast(fp32),
                    ALU.subtract).then_inc(s_g, 1)

            def layer0_steps(q, row):
                if q == 3:
                    norm_in(row)
                if q == 4:
                    norm_out(row)
                if q == 8:
                    make_g(row)
                if q == 10:
                    split_g(row)

            for s, lo, hi in ROWS1:
                with span(dve, lo, hi) as r:
                    row = SB * s + r
                    for q in range(HALVES):
                        split(row * NB, q // 2, q % 2)
                        if s + lo > 0:
                            layer0_steps(q, row - 1)

            START2 = START + 3 * NB

            def add_low(used, row):
                dve.wait_ge(s_used, used)
                dve.wait_ge(s_lowld, 16 * (row - SB + 1))
                dve.wait_ge(s_tr, NB + row)
                nc.vector.tensor_tensor(acc_t[:, :], acc0[:, :], low[:, :], ALU.add).then_inc(s_oa, 1)

            def add_second(used, row):
                dve.wait_ge(s_used, used)
                dve.wait_ge(s_oa, row + 1)
                nc.vector.tensor_tensor(acc_t[:, :], acc1[:, :], acc_t[:, :], ALU.add).then_inc(s_ot, 1)

            def residual(row):
                dve.wait_ge(s_relu, row + 2)
                dve.wait_ge(s_x1ld, 16 * (row + 1))
                nc.vector.tensor_tensor(h[:, :, :], relu_v, x1[:, :, :], ALU.add).then_inc(s_dve, 1)
                statistics(2 * row + START2 + 1)

            def finish(row):
                dve.wait_ge(s_yfree, row + 1)
                normalise(g_raw, s_y, NB + row + 1)

            for s, lo, hi in ROWS2:
                halves = 2 * pass2_tiles(s)
                with span(dve, lo, hi) as r:
                    row = SB * s + r
                    done = pass2_base(s) + r * pass2_tiles(s)
                    for q in range(halves):
                        split(done, q // 2, q % 2)
                        if s + lo == 0:
                            layer0_steps(q, NB - 1)
                        else:
                            if q == 1:
                                add_second(2 * done, row - 1)
                            if q == 5:
                                residual(row - 1)
                            if q == 6:
                                finish(row - 1)
                        if s > 0 and q == min(halves // 2 + 3, halves - 1):
                            add_low(2 * done + halves // 2, row)
            add_second(2 * pass2_base(NS), NB - 1)
            residual(NB - 1)
            finish(NB - 1)

        @block.gpsimd
        def _(pool):
            for free in (s_dinv, s_x1free, s_lowfree, s_yfree):
                pool.sem_inc(free, 1)
            pool.wait_ge(s_fill, 1)

            def row_of(t, row):
                return t[bass.ds(row, 1), :, :].rearrange("o p n -> p (o n)")

            def powers1(row):
                pool.wait_ge(s_stat, row + 1)
                pool.sem_inc(s_apart, 1)
                nc.gpsimd.tensor_scalar(pow_in[:, 0:KC], mean_var[:, :, 1], EPS, None, ALU.add)
                nc.gpsimd.tensor_scalar(deg_pos[:, :], deg[:, :], 0.0, None, ALU.is_gt)
                nc.gpsimd.tensor_scalar(pow_in[:, KC:2 * KC], deg[:, :], TINY, None, ALU.max
                                        ).then_inc(s_pool, 1)
                pool.wait_ge(s_pool, row + 1)
                nc.gpsimd.tensor_tensor(pow_out[:, :], pow_in[:, :], minus_half[:, :], ALU.pow
                                        ).then_inc(s_rstd, 1)
                pool.wait_ge(s_rstd, row + 1)
                nc.gpsimd.tensor_tensor(dinv[:, bass.ds(row * KC, KC)], pow_out[:, KC:2 * KC], deg_pos[:, :],
                                        ALU.mult).then_inc(s_dinv, 1)

            def powers2(row):
                pool.wait_ge(s_stat, NB + row + 1)
                pool.sem_inc(s_apart, 1)
                nc.gpsimd.tensor_scalar(pow_in[:, 0:KC], mean_var[:, :, 1], EPS, None, ALU.add
                                        ).then_inc(s_pool, 1)
                pool.wait_ge(s_pool, NB + row + 1)
                nc.gpsimd.tensor_tensor(pow_out[:, 0:KC], pow_in[:, 0:KC], minus_half[:, 0:KC], ALU.pow
                                        ).then_inc(s_rstd, 1)

            def landed(stored, free, n):
                pool.wait_ge(stored, 16 * (n + 1))
                pool.sem_inc(free, 1)

            def store_x1(row):
                pool.wait_ge(s_x1, row + 1)
                pool.sem_inc(s_apart, 1)
                pool.dma_start(row_of(x1_spill, row), x1[:, :, :].rearrange("p c f -> p (c f)")
                               ).then_inc(s_x1st, 16)

            def load_xt(row):
                pool.wait_ge(s_g, row)
                pool.sem_inc(s_apart, 1)
                pool.dma_start(wide[:, :], x_t[:, bass.ds(row * MB, MB)]).then_inc(s_xt, 16)

            def store_low(row):
                pool.wait_ge(s_lowc, row - SB + 1)
                pool.sem_inc(s_apart, 1)
                pool.dma_start(row_of(low_spill, row), low[:, :]).then_inc(s_lowst, 16)

            for s, lo, hi in ROWS1:
                with span(pool, lo, hi) as r:
                    row = SB * s + r
                    if s + lo > 0:
                        powers1(row - 1)
                        store_x1(row - 1)
                    if s * SB + lo > SB:
                        store_low(row - 1)
                    load_xt(row)
                    if s + lo > 0:
                        landed(s_x1st, s_x1free, row - 1)
                    if s * SB + lo > SB:
                        landed(s_lowst, s_lowfree, row - 1 - SB)
            powers1(NB - 1)
            store_x1(NB - 1)
            store_low(NB - 1)
            landed(s_x1st, s_x1free, NB - 1)
            landed(s_lowst, s_lowfree, NB - 1 - SB)

            def load_x1(row):
                if isinstance(row, int) and row == 0:
                    pool.wait_ge(s_x1p, NB)
                else:
                    pool.wait_ge(s_stat, NB + row)
                    pool.sem_inc(s_apart, 1)
                pool.dma_start(x1[:, :, :].rearrange("p c f -> p (c f)"), row_of(x1_spill, row)
                               ).then_inc(s_x1ld, 16)

            def load_low(row):
                pool.wait_ge(s_oa, row)
                pool.sem_inc(s_apart, 1)
                pool.dma_start(low[:, :], row_of(low_spill, row)).then_inc(s_lowld, 16)

            def store_y(row):
                pool.wait_ge(s_y, row + 1)
                pool.sem_inc(s_apart, 1)
                pool.dma_start(out_v[bass.ds(row, 1), :, :, :].rearrange("o p c f -> p (o c) f"), g_raw
                               ).then_inc(s_yst, 16)

            for s, lo, hi in ROWS2:
                with span(pool, lo, hi) as r:
                    row = SB * s + r
                    if s > 0:
                        load_low(row)
                    if s + lo > 0:
                        powers2(row - 1)
                        store_y(row - 1)
                    load_x1(row)
                    if s + lo > 0:
                        landed(s_yst, s_yfree, row - 1)
            powers2(NB - 1)
            store_y(NB - 1)
            landed(s_yst, s_yfree, NB - 1)

        @block.tensor
        def _(pe):
            pe.wait_ge(s_w, 1)
            for j in range(NB):
                n = j // (NB // XLOADS)
                if j % (NB // XLOADS) == 0:
                    pe.wait_ge(s_raw[n], 16)
                if j >= 2:
                    pe.wait_ge(s_z, j - 1)
                for c in range(KC):
                    k0 = (j * KC + c) * P - n * XCOLS
                    last = nc.tensor.matmul(ps_z[j % 2][:, c * F:(c + 1) * F], raw[:, n, k0:k0 + P], wn_t,
                                            start=True, stop=True)
                last.then_inc(s_zp, 1)

            def high(acc, n, w, first):
                for c in range(HALF):
                    for k, part in enumerate((w[1], w[0])):
                        nc.tensor.matmul(acc[:, :], part[:, c, :], a_hi[:, n, c, :],
                                         start=first and c + k == 0, stop=False)

            def low_part(acc, n, w, final):
                for c in range(HALF):
                    last = nc.tensor.matmul(acc[:, :], w[0][:, c, :], a_lo[:, n, c, :], start=False,
                                            stop=final and c == HALF - 1)
                return last

            def chunks(hi, lo, j, hh):
                return [t[:, j, hh * HALF:(hh + 1) * HALF, :] for t in (hi, lo)]

            def transpose_h(row):
                pe.wait_ge(s_ht, row + 1)
                pe.wait_ge(s_dinv, row + 1)
                for c in range(KC):
                    last = nc.tensor.transpose(ps_tr[:, c * P:(c + 1) * P], acc_t[:, c * P:(c + 1) * P],
                                               ident[:, :])
                last.then_inc(s_tr, 1)

            def transpose_x1(row):
                pe.wait_ge(s_x1, row + 1)
                for c in range(KC):
                    last = nc.tensor.transpose(ps_x1t[:, c * P:(c + 1) * P], x1[:, c, :], ident[:, :])
                last.then_inc(s_x1p, 1)

            def project_x1(row):
                pe.wait_ge(s_x1t, row + 1)
                for c in range(KC):
                    last = nc.tensor.matmul(ps_hw[:, c * F:(c + 1) * F], feat[:, c * P:(c + 1) * P],
                                            w1_sb[:, :], start=True, stop=True)
                last.then_inc(s_hw, 1)

            def layer0_steps(q, row):
                if q == 1:
                    transpose_h(row)
                if q == 4:
                    transpose_x1(row)
                if q == 7:
                    project_x1(row)

            for s, lo, hi in ROWS1:
                with span(pe, lo, hi) as r:
                    row = SB * s + r
                    if s + lo == 0:
                        pe.wait_ge(s_z, NB)
                    else:
                        pe.wait_ge(s_ht, row)
                    for q in range(HALVES):
                        j = NB - 1 - q // 2
                        n = q % RING
                        final = q == HALVES - 1
                        z = chunks(z_hi, z_lo, j, q % 2)
                        pe.wait_ge(s_hi, HALVES * row + q + 1)
                        high(acc0, n, z, q == 0)
                        pe.wait_ge(s_lo, HALVES * row + q + 1)
                        last = low_part(acc0, n, z, False)
                        if final and s == 0:
                            last.then_inc(s_used, 1)
                        if final:
                            pe.wait_ge(s_xt, 16 * (row + 1))
                            nc.tensor.matmul(acc0[:, :], ws_t[:, :], wide[:, :], start=False, stop=True
                                             ).then_inc(s_row, 1)
                        if j < SB * s:
                            first = q == 2 * (NB - SB * s)
                            if first:
                                pe.wait_ge(s_g, SB * s)
                                pe.wait_ge(s_lowc, row - SB)
                            g = chunks(g_hi, g_lo, j, q % 2)
                            high(acc1, n, g, first)
                            last = low_part(acc1, n, g, final)
                        if not (final and s == 0):
                            last.then_inc(s_used, 1)
                        if s + lo > 0:
                            layer0_steps(q, row - 1)

            def transpose_ag(row):
                pe.wait_ge(s_ot, row + 1)
                pe.wait_ge(s_relu, row + 1)
                for c in range(KC):
                    ps = ps_tr[:, c * P:(c + 1) * P]
                    nc.tensor.matmul(ps, acc_t[:, c * P:(c + 1) * P], ident[:, :], start=True, stop=False)
                    for g in (g_lo, g_hi):
                        last = nc.tensor.matmul(ps, ident_r[:, :],
                                                g[:, bass.ds(row, 1), c, :].rearrange("p o f -> p (o f)"),
                                                start=False, stop=g is g_hi)
                last.then_inc(s_tr, 1)

            for s, lo, hi in ROWS2:
                halves = 2 * pass2_tiles(s)
                with span(pe, lo, hi) as r:
                    row = SB * s + r
                    done = pass2_base(s) + r * pass2_tiles(s)
                    for q in range(halves):
                        j = SB * s + q // 2
                        if q == 2 * (NB - 1) and s + lo == 0:
                            pe.wait_ge(s_g, NB)
                        if q == 0 and s + lo == 0:
                            pe.wait_ge(s_ht, NB)
                        elif q == 0:
                            pe.wait_ge(s_oa, row)
                        if q == halves // 2:
                            if s + lo > 0:
                                pe.wait_ge(s_ot, row)
                            else:
                                pe.wait_ge(s_lowc, NB - SB)
                        acc = acc0 if q < halves // 2 else acc1
                        g = chunks(g_hi, g_lo, j, q % 2)
                        pe.wait_ge(s_hi, 2 * done + q + 1)
                        high(acc, q % RING, g, q % (halves // 2) == 0)
                        pe.wait_ge(s_lo, 2 * done + q + 1)
                        low_part(acc, q % RING, g, q % (halves // 2) == halves // 2 - 1).then_inc(s_used, 1)
                        if s + lo == 0:
                            layer0_steps(q, NB - 1)
                        elif q == 3:
                            transpose_ag(row - 1)
            transpose_ag(NB - 1)


def kernel(x, adj, L0_gnn_W, L0_gnn_b, L1_gnn_W, L1_gnn_b):
    import numpy as np
    import concourse.bacc as bacc
    from concourse.bass_utils import run_bass_kernel_spmd

    x, adj, w0, w1, b0, b1 = (np.asarray(a) for a in (x, adj, L0_gnn_W, L1_gnn_W, L0_gnn_b, L1_gnn_b))
    n, nb = x.shape[0], x.shape[0] // MB
    tiles = adj.reshape(nb, MB, nb, KC, P).transpose(0, 2, 4, 3, 1)[:, ::-1]
    arrays = {
        "tiles": np.ascontiguousarray(tiles).reshape(nb * nb, P, KC * MB),
        "x_t": np.ascontiguousarray(x.T),
        "w0_t": np.ascontiguousarray(w0.T),
        "w1_t": np.ascontiguousarray(w1.T),
        "b0": np.ascontiguousarray(b0.reshape(F, 1)),
        "b1": np.ascontiguousarray(b1.reshape(1, F)),
        "eye": np.eye(P, dtype=np.float32),
    }
    nc = bacc.Bacc("TRN2", target_bir_lowering=False, num_devices=1)
    fp32 = mybir.dt.float32
    args = [nc.dram_tensor(name, a.shape, fp32, kind="ExternalInput").ap() for name, a in arrays.items()]
    out = nc.dram_tensor("out", (n, F), fp32, kind="ExternalOutput").ap()
    two_layers(nc, *args, out)
    result = run_bass_kernel_spmd(nc, [arrays], core_ids=[0])
    return result.results[0]["out"]
```

```python
import concourse.bass as bass
from concourse import mybir
from contextlib import ExitStack, nullcontext

P = 128
F = 128
MB = 512
KC = MB // P
SB = 4
RAW = 4
HALF = KC // 2
RING = 4
EPS = 1e-5
TINY = 1.2e-38


def two_layers(nc, tiles, x_t, w0_t, w1_t, b0, b1, eye, out):
    fp32, fp32r = mybir.dt.float32, mybir.dt.float32r
    ALU, ACT = mybir.AluOpType, mybir.ActivationFunctionType
    N = x_t.shape[1]
    NB = N // MB
    NS = NB // SB
    HALVES = 2 * NB
    XLOADS = RAW
    XCOLS = N // XLOADS
    LAST = F - 1

    ROWS1 = [(0, 0, 1), (0, 1, SB), (1, 0, 1), (1, 1, SB)] + [(s, 0, SB) for s in range(2, NS)]
    FIRST = HALVES // 2

    def row_tiles(s):
        return NB + SB * s

    def base1(s):
        return sum(SB * row_tiles(t) for t in range(s))

    def late_rows(s):
        return sum(SB * t for t in range(s))

    def row_halves(s):
        order = [(None, q) for q in range(FIRST)]
        order += [(u, q) for u in range(s) for q in range(2 * SB)]
        order += [(None, q) for q in range(FIRST, HALVES)]
        return [(k, u, q) for k, (u, q) in enumerate(order)]

    def column(q):
        return (q // 2 - SB) % NB

    def releases(s, r):
        return late_rows(s) + r * s + (SB * (s - 1) + r)

    PAIRS = [(0, 1), (1, NB // 2)]
    BASE2 = base1(NS)

    USUAL = dict(add=0, turn=1, low=3, fetch=4, norm=5, scale=7, turn_x1=8, copy_x1=10, project=11, g=13,
                 round=14, split=15)
    EARLY = dict(add=0, turn=1, fetch=2, norm=2, scale=3, low=3, turn_x1=4, copy_x1=5, project=5, g=6,
                 round=7, split=7)
    FINISH = dict(add=0, turn=1, relu=4, residual=5, scale=7)

    def span(eng, lo, hi):
        return nullcontext(lo) if hi - lo == 1 else eng.Fori(lo, hi)

    x1_spill = nc.dram_tensor("x1_spill", (NB, P, KC * F), fp32, kind="Internal").ap()
    low_spill = nc.dram_tensor("low_spill", (NB, P, MB), fp32, kind="Internal").ap()
    out_v = out.rearrange("(i c p) f -> i p c f", c=KC, p=P)

    ctx = ExitStack()
    with ctx:
        def sb(name, shape, dt=fp32):
            return ctx.enter_context(nc.sbuf_tensor(name, shape, dt))

        def pb(name):
            return ctx.enter_context(nc.psum_tensor(name, [P, MB], fp32))

        def sem(name):
            return ctx.enter_context(nc.semaphore(name))

        z_hi = sb("z_hi", [P, NB, KC, F], fp32r)
        z_lo = sb("z_lo", [P, NB, KC, F], fp32r)
        g_hi = sb("g_hi", [P, NB, KC, F], fp32r)
        g_lo = sb("g_lo", [P, NB, KC, F], fp32r)
        raw = sb("raw", [P, RAW, KC * MB])
        a_hi = sb("a_hi", [P, RING, HALF, MB], fp32r)
        a_lo = sb("a_lo", [P, RING, HALF, MB], fp32r)
        acc_t = sb("acc_t", [P, MB])
        feat = sb("feat", [P, KC * F])
        x1 = sb("x1", [P, KC, F])
        h = sb("h", [P, KC, F])
        wide = sb("wide", [P, KC * F])
        low = sb("low", [P, MB])
        ws_t = sb("ws_t", [P, F])
        w1_sb = sb("w1_sb", [P, F])
        ident = sb("ident", [P, P])
        ident_r = sb("ident_r", [P, P], fp32r)
        b1_bc = sb("b1_bc", [P, F])
        b0_col = sb("b0_col", [P, 1])
        b0_last = sb("b0_last", [P, 1])
        stats = sb("stats", [P, KC, 6])
        mean_var = sb("mean_var", [P, KC, 2])
        deg = sb("deg", [P, KC])
        deg_pos = sb("deg_pos", [P, KC])
        pow_in = sb("pow_in", [P, 2 * KC])
        pow_out = sb("pow_out", [P, 2 * KC])
        minus_half = sb("minus_half", [P, 2 * KC])
        dinv = sb("dinv", [P, NB * KC])

        wn_t = feat[:, 0:F]
        g_raw = wide[:, :].rearrange("p (c f) -> p c f", c=KC)
        relu_v = feat[:, :].rearrange("p (c f) -> p c f", c=KC)

        acc0 = pb("acc0")
        acc1 = pb("acc1")
        acc2 = pb("acc2")
        ps_tr = pb("ps_tr")
        ps_x1t = pb("ps_x1t")
        ps_hw = pb("ps_hw")
        ps_z = [pb(f"ps_z{n}") for n in range(2)]
        ps_late = ps_z
        tr_v = ps_tr[:, :].rearrange("p (c f) -> p c f", c=KC)
        hw_v = ps_hw[:, :].rearrange("p (c f) -> p c f", c=KC)

        s_const = sem("const_loaded")
        s_b0 = sem("b0_loaded")
        s_fill = sem("constants_filled")
        s_idr = sem("ident_r_ready")
        s_wnld = sem("wn_loaded")
        s_wn = sem("wn_shifted")
        s_w = sem("weights_shifted")
        s_raw = [sem(f"raw_loaded{n}") for n in range(RAW)]
        s_zp = sem("z_in_psum")
        s_zh = sem("z_hi_ready")
        s_z = sem("z_ready")
        s_hi = sem("a_hi_ready")
        s_lo = sem("a_lo_ready")
        s_used = sem("half_used")
        s_xt = sem("x_t_loaded")
        s_row = sem("layer0_row_done")
        s_ht = sem("h_t_ready")
        s_tr = sem("h_in_psum")
        s_h = sem("h_ready")
        s_stat = sem("stats_ready")
        s_rstd = sem("rstd_ready")
        s_dinv = sem("dinv_ready")
        s_x1 = sem("x1_ready")
        s_x1st = sem("x1_stored")
        s_x1p = sem("x1_t_in_psum")
        s_x1t = sem("x1_t_ready")
        s_hw = sem("hw_in_psum")
        s_gr = sem("g_raw_ready")
        s_gh = sem("g_hi_ready")
        s_g = sem("g_ready")
        s_lowown = sem("own_low_copied")
        s_lowsum = sem("late_low_summed")
        s_lateld = sem("late_low_loaded")
        s_latest = sem("late_low_stored")
        s_lowst = sem("low_stored")
        s_lowld = sem("low_loaded")
        s_oa = sem("first_half_copied")
        s_ot = sem("acc_t_ready")
        s_relu = sem("relu_ready")
        s_x1ld = sem("x1_loaded")
        s_y = sem("y_ready")
        s_x1free = sem("x1_free")
        s_lowfree = sem("low_free")
        s_yfree = sem("y_free")
        s_yst = sem("y_stored")
        s_dve = sem("dve_step")
        s_pool = sem("pool_step")
        s_apart = sem("wait_apart")

        block = ctx.enter_context(nc.Block())

        @block.sync
        def _(sp):
            def load_x(n):
                sp.dma_start(raw[:, n, 0:XCOLS], x_t[:, n * XCOLS:(n + 1) * XCOLS]).then_inc(s_raw[n], 16)

            sp.dma_start(wn_t, w0_t[F:2 * F, :]).then_inc(s_wnld, 16)
            load_x(0)
            sp.dma_start(ws_t[:, :], w0_t[0:F, :]).then_inc(s_const, 16)
            sp.dma_start(w1_sb[:, :], w1_t).then_inc(s_const, 16)
            sp.dma_start(ident[:, :], eye).then_inc(s_const, 16)
            sp.dma_start(b1_bc[:, :], b1.to_broadcast([P, F])).then_inc(s_const, 16)
            sp.dma_start(b0_col[:, :], b0).then_inc(s_const, 16)
            sp.dma_start(b0_last[:, :], b0[LAST:F, :].to_broadcast([P, 1])).then_inc(s_const, 16)
            for n in range(1, XLOADS):
                load_x(n)

            def load(used, n, tile):
                if not (isinstance(used, int) and used == 0):
                    sp.wait_ge(s_lo, 2 * used + 2 * (n - RAW) + 2)
                sp.dma_start(raw[:, n, :], tiles[bass.ds(tile, 1), :, :].rearrange("o p n -> p (o n)")
                             ).then_inc(s_raw[n], 16)

            for n in range(RAW):
                sp.wait_ge(s_zp, (n + 1) * (NB // XLOADS))
                load(0, n, n)
            with sp.Fori(1, SB * NB // RAW) as quad:
                for n in range(RAW):
                    load(quad * RAW, n, quad * RAW + n)
            for s in range(1, NS):
                with sp.Fori(0, SB) as r:
                    used = base1(s) + r * row_tiles(s)
                    row = SB * s + r
                    for k in range(0, row_tiles(s), RAW):
                        late = k // RAW - FIRST // 2 // RAW
                        if late < 0:
                            tile = row * NB + k
                        elif late < s:
                            tile = (SB * late + r) * NB + SB * s
                        else:
                            tile = row * NB + k - RAW * s
                        for n in range(RAW):
                            load(used + k, n, tile + n)
            with sp.Fori(0, NB) as row:
                for n in range(RAW):
                    load(BASE2 + SB * row, n, row * NB + n)

        @block.scalar
        def _(act):
            act.sem_inc(s_relu, 1)
            for j in range(NB):
                act.wait_ge(s_zp, j + 1)
                nc.scalar.activation(z_hi[:, j, :, 0:LAST],
                                     ps_z[j % 2][:, :].rearrange("p (c f) -> p c f", c=KC)[:, :, 0:LAST],
                                     ACT.Copy).then_inc(s_zh, 1)

            act.wait_ge(s_const, 6 * 16)
            nc.scalar.activation(ident_r[:, :], ident[:, :], ACT.Copy).then_inc(s_idr, 1)

            def split(done, t, hh):
                if hh == 0:
                    act.wait_ge(s_raw[t % RAW], (16 // RAW) * done + 16 * (t // RAW + 2))
                q = 2 * done + 2 * t + hh
                if not (isinstance(q, int) and q < RING):
                    act.wait_ge(s_used, q - RING + 1)
                n = (2 * t + hh) % RING
                nc.scalar.activation(a_hi[:, n, :, :],
                                     raw[:, t % RAW, hh * HALF * MB:(hh + 1) * HALF * MB]
                                     .rearrange("p (c m) -> p c m", c=HALF), ACT.Copy).then_inc(s_hi, 1)

            def copy_first(used, row):
                act.wait_ge(s_used, used)
                if not (isinstance(row, int) and row == 0):
                    act.wait_ge(s_tr, row)
                nc.scalar.activation(acc_t[:, :], acc0[:, :], ACT.Identity, bias=b0_col[:, 0:1]
                                     ).then_inc(s_oa, 1)

            def fetch_h(row):
                act.wait_ge(s_tr, row + 1)
                nc.scalar.activation(deg[:, :], tr_v[:, :, LAST], ACT.Copy)
                nc.scalar.activation(h[:, :, 0:LAST], tr_v[:, :, 0:LAST], ACT.Copy).then_inc(s_h, 1)

            def evacuate_x1t(row):
                act.wait_ge(s_x1p, row + 1)
                nc.scalar.activation(feat[:, :], ps_x1t[:, :], ACT.Copy).then_inc(s_x1t, 1)

            def round_g(row):
                act.wait_ge(s_gr, row + 1)
                nc.scalar.activation(g_hi[:, bass.ds(row, 1), :, :].rearrange("p o c f -> p (o c) f"),
                                     g_raw, ACT.Copy).then_inc(s_gh, 1)

            def layer0_steps(when, q, used, low_before, row):
                if q == when["low"] and low_before is not None:
                    act.wait_ge(s_used, used)
                    act.wait_ge(s_lowfree, low_before)
                    nc.scalar.activation(low[:, :], acc1[:, :], ACT.Copy).then_inc(s_lowown, 1)
                if q == when["fetch"]:
                    fetch_h(row)
                if q == when["copy_x1"]:
                    evacuate_x1t(row)
                if q == when["round"]:
                    round_g(row)

            for s, lo, hi in ROWS1:
                with span(act, lo, hi) as r:
                    row = SB * s + r
                    used = base1(s) + r * row_tiles(s)
                    for k, u, q in row_halves(s):
                        split(used, k // 2, k % 2)
                        if u is None and s + lo > 0:
                            layer0_steps(USUAL, q, 2 * used,
                                         releases(s, r) if SB * s + lo > SB else None, row - 1)
                        if u is None and q == FIRST + 2:
                            copy_first(2 * used + FIRST, row)

            def relu(row):
                act.wait_ge(s_tr, NB + row + 1)
                act.wait_ge(s_stat, NB + row)
                for c in range(KC):
                    last = nc.scalar.activation(relu_v[:, c, :], tr_v[:, c, :], ACT.Relu,
                                                scale=dinv[:, bass.ds(row * KC + c, 1)])
                last.then_inc(s_relu, 1)

            for lo, hi in PAIRS:
                with span(act, lo, hi) as pair:
                    for k in range(4 * SB):
                        split(BASE2 + pair * 2 * SB, k // 2, k % 2)
                        row = pair * 2 + k // (2 * SB)
                        q = k % (2 * SB)
                        if lo == 0 and k == q:
                            layer0_steps(EARLY, q, 2 * BASE2, releases(NS, 0), NB - 1)
                        elif q == FINISH["relu"]:
                            relu(row - 1)
            relu(NB - 1)

        @block.vector
        def _(dve):
            steps = [0]

            dve.wait_ge(s_wnld, 16)
            nc.vector.tensor_scalar(wn_t[:, 0:LAST], wn_t[:, 0:LAST], wn_t[:, LAST:F], None, ALU.subtract
                                    ).then_inc(s_wn, 1)
            nc.vector.memset(z_hi[:, :, :, LAST:F].bitcast(fp32), 1.0)
            nc.vector.memset(z_lo[:, :, :, LAST:F].bitcast(fp32), 0.0)
            nc.vector.memset(h[:, :, LAST:F], 0.0)
            nc.vector.memset(minus_half[:, :], -0.5).then_inc(s_fill, 1)
            for j in range(NB):
                dve.wait_ge(s_zh, j + 1)
                nc.vector.tensor_tensor(z_lo[:, j, :, 0:LAST],
                                        ps_z[j % 2][:, :].rearrange("p (c f) -> p c f", c=KC)[:, :, 0:LAST],
                                        z_hi[:, j, :, 0:LAST].bitcast(fp32), ALU.subtract).then_inc(s_z, 1)
            dve.wait_ge(s_const, 6 * 16)
            nc.vector.tensor_scalar(ws_t[:, 0:LAST], ws_t[:, 0:LAST], ws_t[:, LAST:F], None, ALU.subtract)
            nc.vector.tensor_scalar(b0_col[:, :], b0_col[:, :], b0_last[:, 0:1], None, ALU.subtract
                                    ).then_inc(s_dve, 1)
            dve.wait_ge(s_dve, 1)
            nc.vector.tensor_tensor(b0_col[:, :], b0_col[:, :], ident[:, LAST:P], ALU.add)
            nc.vector.memset(ws_t[:, LAST:F], 0.0).then_inc(s_dve, 1)
            dve.wait_ge(s_dve, 2)
            nc.vector.tensor_tensor(ws_t[:, 0:LAST], ws_t[:, 0:LAST], ident[:, 0:LAST], ALU.add
                                    ).then_inc(s_dve, 1)
            dve.wait_ge(s_dve, 3)
            nc.vector.tensor_scalar(ws_t[:, 0:LAST], ws_t[:, 0:LAST], ident[:, LAST:P], None, ALU.subtract
                                    ).then_inc(s_w, 1)

            def split(done, t, hh):
                dve.wait_ge(s_hi, 2 * done + 2 * t + hh + 1)
                n = (2 * t + hh) % RING
                nc.vector.tensor_tensor(a_lo[:, n, :, :],
                                        raw[:, t % RAW, hh * HALF * MB:(hh + 1) * HALF * MB]
                                        .rearrange("p (c m) -> p c m", c=HALF),
                                        a_hi[:, n, :, :].bitcast(fp32), ALU.subtract).then_inc(s_lo, 1)

            START = 3

            def statistics(filled, count, step):
                dve.wait_ge(filled, count)
                for c in range(KC):
                    last = nc.vector.bn_stats(stats[:, c, :], h[:, c, :])
                last.then_inc(s_dve, 1)
                dve.wait_ge(s_dve, step)
                dve.sem_inc(s_apart, 1)
                for c in range(KC):
                    last = nc.vector.bn_aggr(mean_var[:, c, :], stats[:, c, :])
                last.then_inc(s_stat, 1)

            def normalise(dst, signal, count):
                dve.wait_ge(s_rstd, count)
                for c in range(KC):
                    last = nc.vector.tensor_scalar(dst[:, c, :], h[:, c, :], mean_var[:, c, 0:1],
                                                   pow_out[:, c:c + 1], ALU.subtract, ALU.mult)
                last.then_inc(signal, 1)

            def add_second(row):
                dve.wait_ge(s_row, row + 1)
                dve.wait_ge(s_oa, row + 1)
                nc.vector.tensor_tensor(acc_t[:, :], acc2[:, :], acc_t[:, :], ALU.add).then_inc(s_ht, 1)

            def norm_out(row):
                dve.wait_ge(s_x1free, row + 1)
                normalise(x1, s_x1, row + 1)

            def make_g(row):
                dve.wait_ge(s_hw, row + 1)
                nc.vector.tensor_tensor(g_raw, hw_v, b1_bc[:, :].unsqueeze(1).to_broadcast([P, KC, F]),
                                        ALU.add).then_inc(s_dve, 1)
                dve.wait_ge(s_dve, 2 * row + START + 2)
                dve.wait_ge(s_dinv, row + 2)
                nc.vector.tensor_tensor(g_raw, g_raw,
                                        dinv[:, bass.ds(row * KC, KC)].unsqueeze(2).to_broadcast([P, KC, F]),
                                        ALU.mult).then_inc(s_gr, 1)

            def split_g(row):
                dve.wait_ge(s_gh, row + 1)
                nc.vector.tensor_tensor(
                    g_lo[:, bass.ds(row, 1), :, :].rearrange("p o c f -> p (o c) f"), g_raw,
                    g_hi[:, bass.ds(row, 1), :, :].rearrange("p o c f -> p (o c) f").bitcast(fp32),
                    ALU.subtract).then_inc(s_g, 1)

            def layer0_steps(when, q, row):
                if q == when["add"]:
                    add_second(row)
                if q == when["norm"]:
                    statistics(s_h, row + 1, 2 * row + START + 1)
                if q == when["scale"]:
                    norm_out(row)
                if q == when["g"]:
                    make_g(row)
                if q == when["split"]:
                    split_g(row)

            def sum_late(s, r, u, end):
                late = late_rows(s) + r * s + u
                dve.wait_ge(s_used, end)
                if s == 1:
                    dve.wait_ge(s_lowfree, releases(s, r) + 1)
                    nc.vector.tensor_copy(low[:, :], ps_late[u % 2][:, :]).then_inc(s_lowsum, 1)
                else:
                    dve.wait_ge(s_lateld, 16 * (late - SB + 1))
                    nc.vector.tensor_tensor(low[:, :], ps_late[u % 2][:, :], low[:, :], ALU.add
                                            ).then_inc(s_lowsum, 1)

            for s, lo, hi in ROWS1:
                with span(dve, lo, hi) as r:
                    row = SB * s + r
                    used = base1(s) + r * row_tiles(s)
                    for k, u, q in row_halves(s):
                        split(used, k // 2, k % 2)
                        if u is None and s + lo > 0:
                            layer0_steps(USUAL, q, row - 1)
                        if u is not None and u > 0 and q == 2:
                            sum_late(s, r, u - 1, 2 * used + FIRST + 2 * SB * u)
                        if s > 0 and u is None and q == FIRST + 2:
                            sum_late(s, r, s - 1, 2 * used + FIRST + 2 * SB * s)

            START2 = START + 2 * NB

            def add_low(bank, row):
                dve.wait_ge(s_used, 2 * BASE2 + 2 * SB * (row + 1))
                dve.wait_ge(s_lowld, 16 * (row + 1))
                dve.wait_ge(s_tr, NB + row)
                nc.vector.tensor_tensor(acc_t[:, :], bank[:, :], low[:, :], ALU.add).then_inc(s_ot, 1)

            def residual(row):
                dve.wait_ge(s_relu, row + 2)
                dve.wait_ge(s_x1ld, 16 * (row + 1))
                nc.vector.tensor_tensor(h[:, :, :], relu_v, x1[:, :, :], ALU.add).then_inc(s_dve, 1)
                statistics(s_dve, 2 * row + START2 + 1, 2 * row + START2 + 2)

            def finish(row):
                dve.wait_ge(s_yfree, row + 1)
                normalise(g_raw, s_y, NB + row + 1)

            for lo, hi in PAIRS:
                with span(dve, lo, hi) as pair:
                    for k in range(4 * SB):
                        split(BASE2 + pair * 2 * SB, k // 2, k % 2)
                        row = pair * 2 + k // (2 * SB)
                        q = k % (2 * SB)
                        if lo == 0 and k == q:
                            layer0_steps(EARLY, q, NB - 1)
                        else:
                            if q == FINISH["add"]:
                                add_low(acc1 if k == q else acc0, row - 1)
                            if q == FINISH["residual"]:
                                residual(row - 1)
                            if q == FINISH["scale"]:
                                finish(row - 1)
            add_low(acc1, NB - 1)
            residual(NB - 1)
            finish(NB - 1)

        @block.gpsimd
        def _(pool):
            for free in (s_dinv, s_x1free, s_lowfree, s_yfree):
                pool.sem_inc(free, 1)
            pool.wait_ge(s_fill, 1)

            def row_of(t, row):
                return t[bass.ds(row, 1), :, :].rearrange("o p n -> p (o n)")

            def powers1(row):
                pool.wait_ge(s_stat, row + 1)
                pool.sem_inc(s_apart, 1)
                nc.gpsimd.tensor_scalar(pow_in[:, 0:KC], mean_var[:, :, 1], EPS, None, ALU.add)
                nc.gpsimd.tensor_scalar(deg_pos[:, :], deg[:, :], 0.0, None, ALU.is_gt)
                nc.gpsimd.tensor_scalar(pow_in[:, KC:2 * KC], deg[:, :], TINY, None, ALU.max
                                        ).then_inc(s_pool, 1)
                pool.wait_ge(s_pool, row + 1)
                nc.gpsimd.tensor_tensor(pow_out[:, :], pow_in[:, :], minus_half[:, :], ALU.pow
                                        ).then_inc(s_rstd, 1)
                pool.wait_ge(s_rstd, row + 1)
                nc.gpsimd.tensor_tensor(dinv[:, bass.ds(row * KC, KC)], pow_out[:, KC:2 * KC], deg_pos[:, :],
                                        ALU.mult).then_inc(s_dinv, 1)

            def powers2(row):
                pool.wait_ge(s_stat, NB + row + 1)
                pool.sem_inc(s_apart, 1)
                nc.gpsimd.tensor_scalar(pow_in[:, 0:KC], mean_var[:, :, 1], EPS, None, ALU.add
                                        ).then_inc(s_pool, 1)
                pool.wait_ge(s_pool, NB + row + 1)
                nc.gpsimd.tensor_tensor(pow_out[:, 0:KC], pow_in[:, 0:KC], minus_half[:, 0:KC], ALU.pow
                                        ).then_inc(s_rstd, 1)

            def landed(stored, free, n):
                pool.wait_ge(stored, 16 * (n + 1))
                pool.sem_inc(free, 1)

            def store_x1(row):
                pool.wait_ge(s_x1, row + 1)
                pool.sem_inc(s_apart, 1)
                pool.dma_start(row_of(x1_spill, row), x1[:, :, :].rearrange("p c f -> p (c f)")
                               ).then_inc(s_x1st, 16)

            def load_xt(row):
                pool.wait_ge(s_g, row)
                pool.sem_inc(s_apart, 1)
                pool.dma_start(wide[:, :], x_t[:, bass.ds(row * MB, MB)]).then_inc(s_xt, 16)

            def store_own(row):
                pool.wait_ge(s_lowown, row - SB + 1)
                pool.sem_inc(s_apart, 1)
                pool.dma_start(row_of(low_spill, row), low[:, :]).then_inc(s_lowst, 16)
                landed(s_lowst, s_lowfree, row - SB)

            def late(s, r, u):
                n = late_rows(s) + r * s + u
                if s > 1:
                    pool.dma_start(low[:, :], row_of(low_spill, SB * u + r)).then_inc(s_lateld, 16)
                pool.wait_ge(s_lowsum, n + 1)
                pool.sem_inc(s_apart, 1)
                pool.dma_start(row_of(low_spill, SB * u + r), low[:, :]).then_inc(s_latest, 16)
                landed(s_latest, s_lowfree, n)

            for s, lo, hi in ROWS1:
                with span(pool, lo, hi) as r:
                    row = SB * s + r
                    if s + lo > 0:
                        powers1(row - 1)
                        store_x1(row - 1)
                    if s * SB + lo > SB:
                        store_own(row - 1)
                    if s + lo > 0:
                        landed(s_x1st, s_x1free, row - 1)
                    load_xt(row)
                    for u in range(s):
                        late(s, r, u)
            powers1(NB - 1)
            store_x1(NB - 1)
            store_own(NB - 1)
            landed(s_x1st, s_x1free, NB - 1)

            def load_x1(row):
                if isinstance(row, int) and row == 0:
                    pool.wait_ge(s_x1p, NB)
                else:
                    pool.wait_ge(s_stat, NB + row)
                    pool.sem_inc(s_apart, 1)
                pool.dma_start(x1[:, :, :].rearrange("p c f -> p (c f)"), row_of(x1_spill, row)
                               ).then_inc(s_x1ld, 16)

            def load_low(row):
                if not (isinstance(row, int) and row == 0):
                    pool.wait_ge(s_ot, row)
                    pool.sem_inc(s_apart, 1)
                pool.dma_start(low[:, :], row_of(low_spill, row)).then_inc(s_lowld, 16)

            def store_y(row):
                pool.wait_ge(s_y, row + 1)
                pool.sem_inc(s_apart, 1)
                pool.dma_start(out_v[bass.ds(row, 1), :, :, :].rearrange("o p c f -> p (o c) f"), g_raw
                               ).then_inc(s_yst, 16)

            load_low(0)
            load_x1(0)
            with pool.Fori(1, NB) as row:
                load_low(row)
                powers2(row - 1)
                store_y(row - 1)
                load_x1(row)
                landed(s_yst, s_yfree, row - 1)
            powers2(NB - 1)
            store_y(NB - 1)
            landed(s_yst, s_yfree, NB - 1)

        @block.tensor
        def _(pe):
            pe.wait_ge(s_wn, 1)
            for j in range(NB):
                n = j // (NB // XLOADS)
                if j % (NB // XLOADS) == 0:
                    pe.wait_ge(s_raw[n], 16)
                if j >= 2:
                    pe.wait_ge(s_z, j - 1)
                for c in range(KC):
                    k0 = (j * KC + c) * P - n * XCOLS
                    last = nc.tensor.matmul(ps_z[j % 2][:, c * F:(c + 1) * F], raw[:, n, k0:k0 + P], wn_t,
                                            start=True, stop=True)
                last.then_inc(s_zp, 1)

            def high(acc, n, w, first):
                for c in range(HALF):
                    for k, part in enumerate((w[1], w[0])):
                        nc.tensor.matmul(acc[:, :], part[:, c, :], a_hi[:, n, c, :],
                                         start=first and c + k == 0, stop=False)

            def low_part(acc, n, w, final):
                for c in range(HALF):
                    last = nc.tensor.matmul(acc[:, :], w[0][:, c, :], a_lo[:, n, c, :], start=False,
                                            stop=final and c == HALF - 1)
                return last

            def chunks(hi, lo, j, hh):
                return [t[:, j, hh * HALF:(hh + 1) * HALF, :] for t in (hi, lo)]

            def add_x(row):
                pe.wait_ge(s_w, 1)
                pe.wait_ge(s_xt, 16 * (row + 1))
                nc.tensor.matmul(acc2[:, :], ws_t[:, :], wide[:, :], start=False, stop=True
                                 ).then_inc(s_row, 1)

            def transpose_h(row):
                pe.wait_ge(s_ht, row + 1)
                pe.wait_ge(s_dinv, row + 1)
                for c in range(KC):
                    last = nc.tensor.transpose(ps_tr[:, c * P:(c + 1) * P], acc_t[:, c * P:(c + 1) * P],
                                               ident[:, :])
                last.then_inc(s_tr, 1)

            def transpose_x1(row):
                pe.wait_ge(s_x1, row + 1)
                for c in range(KC):
                    last = nc.tensor.transpose(ps_x1t[:, c * P:(c + 1) * P], x1[:, c, :], ident[:, :])
                last.then_inc(s_x1p, 1)

            def project_x1(row):
                pe.wait_ge(s_x1t, row + 1)
                for c in range(KC):
                    last = nc.tensor.matmul(ps_hw[:, c * F:(c + 1) * F], feat[:, c * P:(c + 1) * P],
                                            w1_sb[:, :], start=True, stop=True)
                last.then_inc(s_hw, 1)

            def layer0_steps(when, q, row):
                if q == when["turn"]:
                    transpose_h(row)
                if q == when["turn_x1"]:
                    transpose_x1(row)
                if q == when["project"]:
                    project_x1(row)

            for s, lo, hi in ROWS1:
                with span(pe, lo, hi) as r:
                    row = SB * s + r
                    used = 2 * base1(s) + 2 * row_tiles(s) * r
                    if s + lo == 0:
                        pe.wait_ge(s_z, NB)
                    for k, u, q in row_halves(s):
                        n = k % RING
                        if u is not None:
                            bank = ps_late[u % 2]
                            g = chunks(g_hi, g_lo, SB * (s - 1) + q // 2, q % 2)
                            if u == 0 and q == 0:
                                pe.wait_ge(s_g, SB * s)
                            if q == 0 and SB * s + lo > SB:
                                pe.wait_ge(s_lowsum, late_rows(s) + r * s + max(u - 1, 0))
                            pe.wait_ge(s_hi, used + k + 1)
                            high(bank, n, g, q == 0)
                            pe.wait_ge(s_lo, used + k + 1)
                            low_part(bank, n, g, q == 2 * SB - 1).then_inc(s_used, 1)
                            continue
                        j = column(q)
                        bank = acc0 if q < FIRST else acc2
                        final = q == HALVES - 1
                        if q == 0 and s + lo > 0:
                            pe.wait_ge(s_oa, row)
                        if q == FIRST and s + lo > 0:
                            pe.wait_ge(s_ht, row)
                        z = chunks(z_hi, z_lo, j, q % 2)
                        pe.wait_ge(s_hi, used + k + 1)
                        high(bank, n, z, q % FIRST == 0)
                        pe.wait_ge(s_lo, used + k + 1)
                        last = low_part(bank, n, z, q == FIRST - 1)
                        if j < SB * s:
                            if final:
                                add_x(row)
                            g = chunks(g_hi, g_lo, j, q % 2)
                            if j == 0 and q % 2 == 0:
                                pe.wait_ge(s_g, SB * s - 1)
                                pe.wait_ge(s_lowown, row - SB)
                            if j == SB * s - 1 and q % 2 == 0:
                                pe.wait_ge(s_g, SB * s)
                            high(acc1, n, g, j == 0 and q % 2 == 0)
                            last = low_part(acc1, n, g, j == SB * s - 1 and q % 2 == 1)
                        last.then_inc(s_used, 1)
                        if final and j >= SB * s:
                            add_x(row)
                        if s + lo > 0:
                            layer0_steps(USUAL, q, row - 1)

            def transpose_ag(row):
                pe.wait_ge(s_ot, row + 1)
                pe.wait_ge(s_relu, row + 1)
                for c in range(KC):
                    ps = ps_tr[:, c * P:(c + 1) * P]
                    nc.tensor.matmul(ps, acc_t[:, c * P:(c + 1) * P], ident[:, :], start=True, stop=False)
                    for g in (g_lo, g_hi):
                        last = nc.tensor.matmul(ps, ident_r[:, :],
                                                g[:, bass.ds(row, 1), c, :].rearrange("p o f -> p (o f)"),
                                                start=False, stop=g is g_hi)
                last.then_inc(s_tr, 1)

            for lo, hi in PAIRS:
                with span(pe, lo, hi) as pair:
                    for k in range(4 * SB):
                        row = pair * 2 + k // (2 * SB)
                        q = k % (2 * SB)
                        bank = acc0 if k == q else acc1
                        half = 2 * BASE2 + pair * 4 * SB + k
                        if lo == 0 and k == 0:
                            pe.wait_ge(s_oa, NB)
                        elif lo == 0 and q == 0:
                            pe.wait_ge(s_lowown, NB - SB)
                        elif q == 0:
                            pe.wait_ge(s_ot, row - 1)
                        if lo == 0 and k == 2 * SB - 2:
                            pe.wait_ge(s_g, NB)
                        g = chunks(g_hi, g_lo, NB - SB + q // 2, q % 2)
                        pe.wait_ge(s_hi, half + 1)
                        high(bank, k % RING, g, q == 0)
                        pe.wait_ge(s_lo, half + 1)
                        low_part(bank, k % RING, g, q == 2 * SB - 1).then_inc(s_used, 1)
                        if lo == 0 and k == q:
                            layer0_steps(EARLY, q, NB - 1)
                        elif q == FINISH["turn"]:
                            transpose_ag(row - 1)
            transpose_ag(NB - 1)


def kernel(x, adj, L0_gnn_W, L0_gnn_b, L1_gnn_W, L1_gnn_b):
    import numpy as np
    import concourse.bacc as bacc
    from concourse.bass_utils import run_bass_kernel_spmd

    x, adj, w0, w1, b0, b1 = (np.asarray(a) for a in (x, adj, L0_gnn_W, L1_gnn_W, L0_gnn_b, L1_gnn_b))
    n, nb = x.shape[0], x.shape[0] // MB
    tiles = adj.reshape(nb, MB, nb, KC, P).transpose(0, 2, 4, 3, 1)
    tiles = np.roll(tiles, SB, axis=1)
    arrays = {
        "tiles": np.ascontiguousarray(tiles).reshape(nb * nb, P, KC * MB),
        "x_t": np.ascontiguousarray(x.T),
        "w0_t": np.ascontiguousarray(w0.T),
        "w1_t": np.ascontiguousarray(w1.T),
        "b0": np.ascontiguousarray(b0.reshape(F, 1)),
        "b1": np.ascontiguousarray(b1.reshape(1, F)),
        "eye": np.eye(P, dtype=np.float32),
    }
    nc = bacc.Bacc("TRN2", target_bir_lowering=False, num_devices=1)
    fp32 = mybir.dt.float32
    args = [nc.dram_tensor(name, a.shape, fp32, kind="ExternalInput").ap() for name, a in arrays.items()]
    out = nc.dram_tensor("out", (n, F), fp32, kind="ExternalOutput").ap()
    two_layers(nc, *args, out)
    result = run_bass_kernel_spmd(nc, [arrays], core_ids=[0])
    return result.results[0]["out"]
```

```python
import concourse.bass as bass
from concourse import mybir
from contextlib import ExitStack, nullcontext

P = 128
F = 128
MB = 512
KC = MB // P
SB = 4
RAW = 4
HALF = KC // 2
RING = 4
EPS = 1e-5
TINY = 1.2e-38


def two_layers(nc, tiles, x_t, w0_t, w1_t, b0, b1, eye, out):
    fp32, fp32r = mybir.dt.float32, mybir.dt.float32r
    ALU, ACT = mybir.AluOpType, mybir.ActivationFunctionType
    N = x_t.shape[1]
    NB = N // MB
    NS = NB // SB
    HALVES = 2 * NB
    XLOADS = RAW
    XCOLS = N // XLOADS
    LAST = F - 1

    ROWS1 = [(0, 0, 1), (0, 1, SB), (1, 0, 1), (1, 1, SB)] + [(s, 0, SB) for s in range(2, NS)]
    FIRST = HALVES // 2
    LATE_SUM = 3
    BETWEEN = 4

    def row_tiles(s):
        return NB + SB * s

    def base1(s):
        return sum(SB * row_tiles(t) for t in range(s))

    def late_rows(s):
        return sum(SB * t for t in range(s))

    def row_halves(s):
        order = [(None, q) for q in range(FIRST)]
        own = FIRST
        for u in range(s):
            if u > 0:
                order += [(None, q) for q in range(own, own + BETWEEN)]
                own += BETWEEN
            order += [(u, q) for q in range(2 * SB)]
        order += [(None, q) for q in range(own, HALVES)]
        return [(k, u, q) for k, (u, q) in enumerate(order)]

    def place(s, u, q):
        return next(k for k, *half in row_halves(s) if half == [u, q])

    def column(q):
        return (q // 2 - SB) % NB

    def releases(s, r):
        return late_rows(s) + r * s + (SB * (s - 1) + r)

    PAIRS = [(0, 1), (1, NB // 2)]
    BASE2 = base1(NS)

    USUAL = dict(add=2, turn=3, low=5, fetch=7, norm=7, scale=10, g=11, round=12, split=13)
    EARLY = dict(add=0, turn=1, fetch=4, norm=4, low=5, g=6, scale=6, round=7, split=7)
    FINISH = dict(add=1, turn=2, relu=6, residual=6, scale=10)

    def pair_halves(first):
        order = [(0, q) for q in range(2 * SB)] + [(1, q) for q in range(2 * SB)]
        if first:
            row0, row1 = order[:2 * SB], order[2 * SB:]
            order = row0[:-2] + row1[:2] + row0[-2:] + row1[2:]
        return [(k, row, q) for k, (row, q) in enumerate(order)]

    def finish_steps(first, k, pair):
        steps = []
        for name, after in FINISH.items():
            if first:
                if k == 2 * SB + 2 + after:
                    steps.append((name, 0))
            elif k % (2 * SB) == after % (2 * SB):
                steps.append((name, pair * 2 + k // (2 * SB) - 1 - after // (2 * SB)))
        return steps[::-1]

    LEFT0 = [name for name, after in FINISH.items() if 4 * SB <= 2 * SB + 2 + after and after < 2 * SB]
    LEFT_LAST = [name for name, after in FINISH.items() if after >= 2 * SB]

    def span(eng, lo, hi):
        return nullcontext(lo) if hi - lo == 1 else eng.Fori(lo, hi)

    x1_spill = nc.dram_tensor("x1_spill", (NB, P, KC * F), fp32, kind="Internal").ap()
    low_spill = nc.dram_tensor("low_spill", (NB, P, MB), fp32, kind="Internal").ap()
    out_v = out.rearrange("(i c p) f -> i p c f", c=KC, p=P)

    ctx = ExitStack()
    with ctx:
        def sb(name, shape, dt=fp32):
            return ctx.enter_context(nc.sbuf_tensor(name, shape, dt))

        def pb(name):
            return ctx.enter_context(nc.psum_tensor(name, [P, MB], fp32))

        def sem(name):
            return ctx.enter_context(nc.semaphore(name))

        z_hi = sb("z_hi", [P, NB, KC, F], fp32r)
        z_lo = sb("z_lo", [P, NB, KC, F], fp32r)
        g_hi = sb("g_hi", [P, NB, KC, F], fp32r)
        g_lo = sb("g_lo", [P, NB, KC, F], fp32r)
        raw = sb("raw", [P, RAW, KC * MB])
        a_hi = sb("a_hi", [P, RING, HALF, MB], fp32r)
        a_lo = sb("a_lo", [P, RING, HALF, MB], fp32r)
        acc_t = sb("acc_t", [P, MB])
        feat = sb("feat", [P, KC * F])
        x1 = sb("x1", [P, KC, F])
        h = sb("h", [P, KC, F])
        wide = sb("wide", [P, KC * F])
        low = sb("low", [P, MB])
        ws_t = sb("ws_t", [P, F])
        w1_sb = sb("w1_sb", [P, F])
        ident = sb("ident", [P, P])
        ident_r = sb("ident_r", [P, P], fp32r)
        averager = sb("averager", [P, P])
        not_last = sb("not_last", [P, 1])
        b1_bc = sb("b1_bc", [P, F])
        b0_col = sb("b0_col", [P, 1])
        b0_last = sb("b0_last", [P, 1])
        stats = sb("stats", [P, KC, 6])
        mean_var = sb("mean_var", [P, KC, 2])
        deg = sb("deg", [P, KC])
        deg_pos = sb("deg_pos", [P, KC])
        pow_in = sb("pow_in", [P, 2 * KC])
        pow_out = sb("pow_out", [P, 2 * KC])
        shift = sb("shift", [P, KC])
        minus_half = sb("minus_half", [P, 2 * KC])
        dinv = sb("dinv", [P, NB * KC])

        wn_t = feat[:, 0:F]
        g_raw = wide[:, :].rearrange("p (c f) -> p c f", c=KC)
        x1_back = z_hi[:, :, :, :].bitcast(fp32)
        low_back = z_lo[:, :, :, :].bitcast(fp32).rearrange("p j c f -> p j (c f)")
        relu_v = feat[:, :].rearrange("p (c f) -> p c f", c=KC)

        acc0 = pb("acc0")
        acc1 = pb("acc1")
        acc2 = pb("acc2")
        ps_tr = pb("ps_tr")
        ps_hw = pb("ps_hw")
        ps_mean = pb("ps_mean")
        ps_late = [pb(f"ps_late{n}") for n in range(2)]
        ps_z = [*ps_late, ps_tr, ps_hw]
        ps_z_v = [t[:, :].rearrange("p (c f) -> p c f", c=KC) for t in ps_z]
        tr_v = ps_tr[:, :].rearrange("p (c f) -> p c f", c=KC)
        hw_v = ps_hw[:, :].rearrange("p (c f) -> p c f", c=KC)

        s_const = sem("const_loaded")
        s_fill = sem("constants_filled")
        s_idr = sem("ident_r_ready")
        s_wnld = sem("wn_loaded")
        s_wn = sem("wn_shifted")
        s_w = sem("weights_shifted")
        s_raw = [sem(f"raw_loaded{n}") for n in range(RAW)]
        s_zp = sem("z_in_psum")
        s_zh = sem("z_hi_ready")
        s_z = sem("z_ready")
        s_hi = sem("a_hi_ready")
        s_lo = sem("a_lo_ready")
        s_used = sem("half_used")
        s_xt = sem("x_t_loaded")
        s_row = sem("layer0_row_done")
        s_ht = sem("h_t_ready")
        s_tr = sem("h_in_psum")
        s_h = sem("h_ready")
        s_stat = sem("stats_ready")
        s_rstd = sem("rstd_ready")
        s_dinv = sem("dinv_ready")
        s_x1 = sem("x1_ready")
        s_x1st = sem("x1_stored")
        s_hw = sem("hw_in_psum")
        s_gr = sem("g_raw_ready")
        s_gh = sem("g_hi_ready")
        s_g = sem("g_ready")
        s_lowown = sem("own_low_copied")
        s_lowsum = sem("late_low_summed")
        s_lateld = sem("late_low_loaded")
        s_latest = sem("late_low_stored")
        s_lowst = sem("low_stored")
        s_back = sem("x1_and_low_back")
        s_wmean = sem("w1_mean_in_psum")
        s_oa = sem("first_half_copied")
        s_ot = sem("acc_t_ready")
        s_relu = sem("relu_ready")
        s_y = sem("y_ready")
        s_x1free = sem("x1_free")
        s_lowfree = sem("low_free")
        s_yfree = sem("y_free")
        s_yst = sem("y_stored")
        s_ylast = sem("last_y_stored")
        s_dve = sem("dve_step")
        s_pool = sem("pool_step")
        s_apart = sem("wait_apart")

        block = ctx.enter_context(nc.Block())

        @block.sync
        def _(sp):
            def load_x(n):
                sp.dma_start(raw[:, n, 0:XCOLS], x_t[:, n * XCOLS:(n + 1) * XCOLS]).then_inc(s_raw[n], 16)

            sp.dma_start(wn_t, w0_t[F:2 * F, :]).then_inc(s_wnld, 16)
            load_x(0)
            sp.dma_start(ws_t[:, :], w0_t[0:F, :]).then_inc(s_const, 16)
            sp.dma_start(w1_sb[:, :], w1_t).then_inc(s_const, 16)
            sp.dma_start(ident[:, :], eye).then_inc(s_const, 16)
            sp.dma_start(b1_bc[:, :], b1.to_broadcast([P, F])).then_inc(s_const, 16)
            sp.dma_start(b0_col[:, :], b0).then_inc(s_const, 16)
            sp.dma_start(b0_last[:, :], b0[LAST:F, :].to_broadcast([P, 1])).then_inc(s_const, 16)
            for n in range(1, XLOADS):
                load_x(n)

            def load(used, n, tile):
                if not (isinstance(used, int) and used == 0):
                    sp.wait_ge(s_lo, 2 * used + 2 * (n - RAW) + 2)
                sp.dma_start(raw[:, n, :], tiles[bass.ds(tile, 1), :, :].rearrange("o p n -> p (o n)")
                             ).then_inc(s_raw[n], 16)

            for n in range(RAW):
                sp.wait_ge(s_zp, (n + 1) * (NB // XLOADS))
                load(0, n, n)
            with sp.Fori(1, SB * NB // RAW) as quad:
                for n in range(RAW):
                    load(quad * RAW, n, quad * RAW + n)
            for s in range(1, NS):
                with sp.Fori(0, SB) as r:
                    used = base1(s) + r * row_tiles(s)
                    row = SB * s + r
                    for k, u, q in row_halves(s)[::2]:
                        t = k // 2
                        tile = row * NB + q // 2 if u is None else (SB * u + r) * NB + SB * s + q // 2
                        load(used + t - t % RAW, t % RAW, tile)
            for k, row, q in pair_halves(True)[::2]:
                used = BASE2 + k // 2
                load(used - used % RAW, used % RAW, row * NB + q // 2)
            with sp.Fori(2, NB) as row:
                for n in range(RAW):
                    load(BASE2 + SB * row, n, row * NB + n)
            sp.wait_ge(s_y, NB)
            sp.dma_start(out_v[NB - 1, :, :, :], g_raw).then_inc(s_ylast, 16)
            sp.wait_ge(s_ylast, 16)

        @block.scalar
        def _(act):
            act.sem_inc(s_relu, 1)
            for j in range(NB):
                act.wait_ge(s_zp, j + 1)
                nc.scalar.activation(z_hi[:, j, :, 0:LAST],
                                     ps_z_v[j % len(ps_z)][:, :, 0:LAST],
                                     ACT.Copy).then_inc(s_zh, 1)

            act.wait_ge(s_const, 6 * 16)
            nc.scalar.activation(ident_r[:, :], ident[:, :], ACT.Copy).then_inc(s_idr, 1)

            def split(done, t, hh):
                if hh == 0:
                    act.wait_ge(s_raw[t % RAW], (16 // RAW) * done + 16 * (t // RAW + 2))
                q = 2 * done + 2 * t + hh
                if not (isinstance(q, int) and q < RING):
                    act.wait_ge(s_used, q - RING + 1)
                n = (2 * t + hh) % RING
                nc.scalar.activation(a_hi[:, n, :, :],
                                     raw[:, t % RAW, hh * HALF * MB:(hh + 1) * HALF * MB]
                                     .rearrange("p (c m) -> p c m", c=HALF), ACT.Copy).then_inc(s_hi, 1)

            def copy_first(used, row):
                act.wait_ge(s_used, used)
                if not (isinstance(row, int) and row == 0):
                    act.wait_ge(s_hw, row)
                nc.scalar.activation(acc_t[:, :], acc0[:, :], ACT.Identity, bias=b0_col[:, 0:1]
                                     ).then_inc(s_oa, 1)

            def fetch_h(row):
                act.wait_ge(s_tr, row + 1)
                nc.scalar.activation(deg[:, :], tr_v[:, :, LAST], ACT.Copy)
                nc.scalar.activation(h[:, :, 0:LAST], tr_v[:, :, 0:LAST], ACT.Copy).then_inc(s_h, 1)

            def round_g(row):
                act.wait_ge(s_gr, row + 1)
                nc.scalar.activation(g_hi[:, bass.ds(row, 1), :, :].rearrange("p o c f -> p (o c) f"),
                                     g_raw, ACT.Copy).then_inc(s_gh, 1)

            def layer0_steps(when, q, used, low_before, row):
                if q == when["low"] and low_before is not None:
                    act.wait_ge(s_used, used)
                    act.wait_ge(s_lowfree, low_before)
                    nc.scalar.activation(low[:, :], acc1[:, :], ACT.Copy).then_inc(s_lowown, 1)
                if q == when["fetch"]:
                    fetch_h(row)
                if q == when["round"]:
                    round_g(row)

            for s, lo, hi in ROWS1:
                with span(act, lo, hi) as r:
                    row = SB * s + r
                    used = base1(s) + r * row_tiles(s)
                    for k, u, q in row_halves(s):
                        split(used, k // 2, k % 2)
                        if u is None and s + lo > 0:
                            layer0_steps(USUAL, q, 2 * used,
                                         releases(s, r) if SB * s + lo > SB else None, row - 1)
                        if u is None and q == FIRST + 2:
                            copy_first(2 * used + FIRST, row)

            def relu(row):
                act.wait_ge(s_tr, NB + row + 1)
                act.wait_ge(s_stat, NB + row)
                for c in range(KC):
                    last = nc.scalar.activation(relu_v[:, c, :], tr_v[:, c, :], ACT.Relu,
                                                scale=dinv[:, bass.ds(row * KC + c, 1)])
                last.then_inc(s_relu, 1)

            def finish(row):
                act.wait_ge(s_rstd, NB + row + 1)
                act.wait_ge(s_yfree, row + 1)
                for c in range(KC):
                    last = nc.scalar.activation(g_raw[:, c, :], h[:, c, :], ACT.Identity,
                                                bias=shift[:, c:c + 1], scale=pow_out[:, c:c + 1])
                last.then_inc(s_y, 1)

            for lo, hi in PAIRS:
                first = lo == 0
                with span(act, lo, hi) as pair:
                    for k, _, _ in pair_halves(first):
                        split(BASE2 + pair * 2 * SB, k // 2, k % 2)
                        if first:
                            layer0_steps(EARLY, k, 2 * BASE2, releases(NS, 0), NB - 1)
                        for name, row in finish_steps(first, k, pair):
                            if name == "relu":
                                relu(row)
                            if name == "scale":
                                finish(row)
                    if first and "relu" in LEFT0:
                        relu(0)
                    if first and "scale" in LEFT0:
                        finish(0)
            if "scale" in LEFT_LAST:
                finish(NB - 2)
            relu(NB - 1)

        @block.vector
        def _(dve):
            dve.wait_ge(s_wnld, 16)
            nc.vector.tensor_scalar(wn_t[:, 0:LAST], wn_t[:, 0:LAST], wn_t[:, LAST:F], None, ALU.subtract
                                    ).then_inc(s_wn, 1)
            nc.vector.memset(z_hi[:, :, :, LAST:F].bitcast(fp32), 1.0)
            nc.vector.memset(z_lo[:, :, :, LAST:F].bitcast(fp32), 0.0)
            nc.vector.memset(h[:, :, LAST:F], 0.0)
            nc.vector.memset(averager[:, :], 1.0 / F)
            nc.vector.memset(minus_half[:, :], -0.5).then_inc(s_fill, 1)
            for j in range(NB):
                dve.wait_ge(s_zh, j + 1)
                nc.vector.tensor_tensor(z_lo[:, j, :, 0:LAST],
                                        ps_z_v[j % len(ps_z)][:, :, 0:LAST],
                                        z_hi[:, j, :, 0:LAST].bitcast(fp32), ALU.subtract).then_inc(s_z, 1)

            def prepare_weights():
                dve.wait_ge(s_const, 6 * 16)
                nc.vector.tensor_scalar(ws_t[:, 0:LAST], ws_t[:, 0:LAST], ws_t[:, LAST:F], None, ALU.subtract)
                nc.vector.tensor_scalar(not_last[:, :], ident[:, LAST:P], -1.0, 1.0, ALU.mult, ALU.add)
                nc.vector.tensor_scalar(b0_col[:, :], b0_col[:, :], b0_last[:, 0:1], None, ALU.subtract
                                        ).then_inc(s_dve, 1)
                dve.wait_ge(s_dve, 1)
                nc.vector.tensor_tensor(b0_col[:, :], b0_col[:, :], ident[:, LAST:P], ALU.add)
                nc.vector.memset(ws_t[:, LAST:F], 0.0).then_inc(s_dve, 1)
                dve.wait_ge(s_dve, 2)
                nc.vector.tensor_tensor(ws_t[:, 0:LAST], ws_t[:, 0:LAST], ident[:, 0:LAST], ALU.add
                                        ).then_inc(s_dve, 1)
                dve.wait_ge(s_dve, 3)
                nc.vector.tensor_scalar(ws_t[:, 0:LAST], ws_t[:, 0:LAST], ident[:, LAST:P], None, ALU.subtract)
                dve.wait_ge(s_wmean, 1)
                nc.vector.tensor_tensor(w1_sb[:, :], w1_sb[:, :], ps_mean[:, 0:F], ALU.subtract
                                        ).then_inc(s_dve, 1)
                dve.wait_ge(s_dve, 4)
                nc.vector.tensor_scalar(w1_sb[:, :], w1_sb[:, :], not_last[:, 0:1], None, ALU.mult
                                        ).then_inc(s_w, 1)

            def split(done, t, hh):
                dve.wait_ge(s_hi, 2 * done + 2 * t + hh + 1)
                n = (2 * t + hh) % RING
                nc.vector.tensor_tensor(a_lo[:, n, :, :],
                                        raw[:, t % RAW, hh * HALF * MB:(hh + 1) * HALF * MB]
                                        .rearrange("p (c m) -> p c m", c=HALF),
                                        a_hi[:, n, :, :].bitcast(fp32), ALU.subtract).then_inc(s_lo, 1)

            START = 4

            def statistics(filled, count, step):
                dve.wait_ge(filled, count)
                for c in range(KC):
                    last = nc.vector.bn_stats(stats[:, c, :], h[:, c, :])
                last.then_inc(s_dve, 1)
                dve.wait_ge(s_dve, step)
                dve.sem_inc(s_apart, 1)
                for c in range(KC):
                    last = nc.vector.bn_aggr(mean_var[:, c, :], stats[:, c, :])
                last.then_inc(s_stat, 1)

            def normalise(dst, signal, count):
                dve.wait_ge(s_rstd, count)
                for c in range(KC):
                    last = nc.vector.tensor_scalar(dst[:, c, :], h[:, c, :], mean_var[:, c, 0:1],
                                                   pow_out[:, c:c + 1], ALU.subtract, ALU.mult)
                last.then_inc(signal, 1)

            def add_second(row):
                dve.wait_ge(s_row, row + 1)
                dve.wait_ge(s_oa, row + 1)
                nc.vector.tensor_tensor(acc_t[:, :], acc2[:, :], acc_t[:, :], ALU.add).then_inc(s_ht, 1)

            def norm_out(row):
                dve.wait_ge(s_x1free, row + 1)
                normalise(x1, s_x1, row + 1)

            def make_g(row):
                dve.wait_ge(s_hw, row + 1)
                dve.wait_ge(s_rstd, row + 1)
                for c in range(KC):
                    last = nc.vector.scalar_tensor_tensor(g_raw[:, c, :], hw_v[:, c, :], pow_out[:, c:c + 1],
                                                          b1_bc[:, :], ALU.mult, ALU.add)
                last.then_inc(s_dve, 1)
                dve.wait_ge(s_dve, 2 * row + START + 2)
                dve.wait_ge(s_dinv, row + 2)
                nc.vector.tensor_tensor(g_raw, g_raw,
                                        dinv[:, bass.ds(row * KC, KC)].unsqueeze(2).to_broadcast([P, KC, F]),
                                        ALU.mult).then_inc(s_gr, 1)

            def split_g(row):
                dve.wait_ge(s_gh, row + 1)
                nc.vector.tensor_tensor(
                    g_lo[:, bass.ds(row, 1), :, :].rearrange("p o c f -> p (o c) f"), g_raw,
                    g_hi[:, bass.ds(row, 1), :, :].rearrange("p o c f -> p (o c) f").bitcast(fp32),
                    ALU.subtract).then_inc(s_g, 1)

            def layer0_steps(when, q, row):
                if q == when["add"]:
                    add_second(row)
                if q == when["norm"]:
                    statistics(s_h, row + 1, 2 * row + START + 1)
                if q == when["scale"]:
                    norm_out(row)
                if q == when["g"]:
                    make_g(row)
                if q == when["split"]:
                    split_g(row)

            def sum_late(s, r, u, end):
                late = late_rows(s) + r * s + u
                dve.wait_ge(s_used, end)
                if s == 1:
                    dve.wait_ge(s_lowfree, releases(s, r) + 1)
                    nc.vector.tensor_copy(low[:, :], ps_late[u % 2][:, :]).then_inc(s_lowsum, 1)
                else:
                    dve.wait_ge(s_lateld, 16 * (late - SB + 1))
                    nc.vector.tensor_tensor(low[:, :], ps_late[u % 2][:, :], low[:, :], ALU.add
                                            ).then_inc(s_lowsum, 1)

            for s, lo, hi in ROWS1:
                with span(dve, lo, hi) as r:
                    row = SB * s + r
                    used = base1(s) + r * row_tiles(s)
                    for k, u, q in row_halves(s):
                        split(used, k // 2, k % 2)
                        if s + lo == 0 and q == FIRST // 2:
                            prepare_weights()
                        if u is None and s + lo > 0:
                            layer0_steps(USUAL, q, row - 1)
                        for v in range(s):
                            end = place(s, v, 2 * SB - 1)
                            if k == end + LATE_SUM:
                                sum_late(s, r, v, 2 * used + end + 1)

            START2 = START + 2 * NB

            def add_low(bank, used, row):
                dve.wait_ge(s_used, used)
                dve.wait_ge(s_tr, NB + row)
                before = low[:, :].unsqueeze(1)
                if not (isinstance(row, int) and row == NB - 1):
                    before = low_back[:, bass.ds(row, 1), :]
                nc.vector.tensor_tensor(acc_t[:, :].unsqueeze(1), bank[:, :].unsqueeze(1), before, ALU.add
                                        ).then_inc(s_ot, 1)

            def residual(row):
                dve.wait_ge(s_relu, row + 2)
                if not (isinstance(row, int) and row == 0):
                    dve.wait_ge(s_y, row)
                from_x1 = x1[:, :, :]
                if not (isinstance(row, int) and row == NB - 1):
                    from_x1 = x1_back[:, bass.ds(row, 1), :, :].rearrange("p o c f -> p (o c) f")
                nc.vector.tensor_tensor(h[:, :, :], relu_v, from_x1, ALU.add).then_inc(s_dve, 1)
                statistics(s_dve, 2 * row + START2 + 1, 2 * row + START2 + 2)

            for lo, hi in PAIRS:
                first = lo == 0
                with span(dve, lo, hi) as pair:
                    base = 2 * BASE2 + pair * 4 * SB
                    for k, _, _ in pair_halves(first):
                        split(BASE2 + pair * 2 * SB, k // 2, k % 2)
                        if first:
                            layer0_steps(EARLY, k, NB - 1)
                        for name, row in finish_steps(first, k, pair):
                            if name == "add":
                                if first:
                                    dve.wait_ge(s_back, 2 * 16 * (NB - 1))
                                bank = acc0 if first or k >= 2 * SB else acc1
                                add_low(bank, base + k - FINISH["add"], row)
                            if name == "residual":
                                residual(row)
                    if first and "residual" in LEFT0:
                        residual(0)
            dve.wait_ge(s_lowown, NB - SB)
            add_low(acc1, 2 * BASE2 + 2 * SB * NB, NB - 1)
            residual(NB - 1)
            dve.wait_ge(s_yfree, NB)
            normalise(g_raw, s_y, 2 * NB)

        @block.gpsimd
        def _(pool):
            for free in (s_dinv, s_x1free, s_lowfree, s_yfree):
                pool.sem_inc(free, 1)
            pool.wait_ge(s_fill, 1)

            def row_of(t, row):
                return t[bass.ds(row, 1), :, :].rearrange("o p n -> p (o n)")

            def powers1(row):
                pool.wait_ge(s_stat, row + 1)
                pool.sem_inc(s_apart, 1)
                nc.gpsimd.tensor_scalar(pow_in[:, 0:KC], mean_var[:, :, 1], EPS, None, ALU.add)
                nc.gpsimd.tensor_scalar(deg_pos[:, :], deg[:, :], 0.0, None, ALU.is_gt)
                nc.gpsimd.tensor_scalar(pow_in[:, KC:2 * KC], deg[:, :], TINY, None, ALU.max
                                        ).then_inc(s_pool, 1)
                pool.wait_ge(s_pool, row + 1)
                nc.gpsimd.tensor_tensor(pow_out[:, :], pow_in[:, :], minus_half[:, :], ALU.pow
                                        ).then_inc(s_rstd, 1)
                pool.wait_ge(s_rstd, row + 1)
                nc.gpsimd.tensor_tensor(dinv[:, bass.ds(row * KC, KC)], pow_out[:, KC:2 * KC], deg_pos[:, :],
                                        ALU.mult).then_inc(s_dinv, 1)

            def powers2(row):
                pool.wait_ge(s_stat, NB + row + 1)
                pool.sem_inc(s_apart, 1)
                nc.gpsimd.tensor_scalar(shift[:, :], mean_var[:, :, 0], -1.0, None, ALU.mult)
                nc.gpsimd.tensor_scalar(pow_in[:, 0:KC], mean_var[:, :, 1], EPS, None, ALU.add
                                        ).then_inc(s_pool, 1)
                pool.wait_ge(s_pool, NB + 2 * row + 1)
                nc.gpsimd.tensor_tensor(pow_out[:, 0:KC], pow_in[:, 0:KC], minus_half[:, 0:KC], ALU.pow
                                        ).then_inc(s_pool, 1)
                pool.wait_ge(s_pool, NB + 2 * row + 2)
                nc.gpsimd.tensor_tensor(shift[:, :], shift[:, :], pow_out[:, 0:KC], ALU.mult
                                        ).then_inc(s_rstd, 1)

            def landed(stored, free, n):
                pool.wait_ge(stored, 16 * (n + 1))
                pool.sem_inc(free, 1)

            def store_x1(row):
                pool.wait_ge(s_x1, row + 1)
                pool.sem_inc(s_apart, 1)
                pool.dma_start(row_of(x1_spill, row), x1[:, :, :].rearrange("p c f -> p (c f)")
                               ).then_inc(s_x1st, 16)

            def load_xt(row):
                pool.wait_ge(s_g, row)
                pool.sem_inc(s_apart, 1)
                pool.dma_start(wide[:, :], x_t[:, bass.ds(row * MB, MB)]).then_inc(s_xt, 16)

            def store_own(row):
                pool.wait_ge(s_lowown, row - SB + 1)
                pool.sem_inc(s_apart, 1)
                pool.dma_start(row_of(low_spill, row), low[:, :]).then_inc(s_lowst, 16)
                landed(s_lowst, s_lowfree, row - SB)

            def late(s, r, u):
                n = late_rows(s) + r * s + u
                if s > 1:
                    pool.dma_start(low[:, :], row_of(low_spill, SB * u + r)).then_inc(s_lateld, 16)
                pool.wait_ge(s_lowsum, n + 1)
                pool.sem_inc(s_apart, 1)
                pool.dma_start(row_of(low_spill, SB * u + r), low[:, :]).then_inc(s_latest, 16)
                landed(s_latest, s_lowfree, n)

            def bring_back(halves, used):
                for q in halves:
                    j = column(q)
                    if j == NB - 1:
                        continue
                    pool.wait_ge(s_used, used + place(NS - 1, None, q + 1) + 1)
                    pool.dma_start(x1_back[:, j, :, :].rearrange("p c f -> p (c f)"), x1_spill[j, :, :]
                                   ).then_inc(s_back, 16)
                    pool.dma_start(low_back[:, j, :], low_spill[j, :, :]).then_inc(s_back, 16)

            for s, lo, hi in ROWS1[:-1] + [(NS - 1, 0, SB - 1), (NS - 1, SB - 1, SB)]:
                with span(pool, lo, hi) as r:
                    row = SB * s + r
                    bringing = lo == SB - 1 and s == NS - 1
                    used = 2 * base1(NS - 1) + 2 * (SB - 1) * row_tiles(NS - 1)
                    if s + lo > 0:
                        powers1(row - 1)
                        store_x1(row - 1)
                    if s * SB + lo > SB:
                        store_own(row - 1)
                    if s + lo > 0:
                        landed(s_x1st, s_x1free, row - 1)
                    load_xt(row)
                    if bringing:
                        bring_back(range(0, 2 * SB, 2), used)
                    until = [FIRST + BETWEEN * u for u in range(s - 1)] + [HALVES]
                    for u in range(s):
                        late(s, r, u)
                        if bringing:
                            bring_back(range(until[u - 1] if u > 0 else 2 * SB, until[u], 2), used)
            powers1(NB - 1)

            def store_y(row):
                pool.wait_ge(s_y, row + 1)
                pool.sem_inc(s_apart, 1)
                pool.dma_start(out_v[bass.ds(row, 1), :, :, :].rearrange("o p c f -> p (o c) f"), g_raw
                               ).then_inc(s_yst, 16)

            with pool.Fori(0, NB - 1) as row:
                powers2(row)
                store_y(row)
                landed(s_yst, s_yfree, row)
            powers2(NB - 1)

        @block.tensor
        def _(pe):
            pe.wait_ge(s_wn, 1)
            for j in range(NB):
                n = j // (NB // XLOADS)
                if j % (NB // XLOADS) == 0:
                    pe.wait_ge(s_raw[n], 16)
                if j >= len(ps_z):
                    pe.wait_ge(s_z, j - len(ps_z) + 1)
                for c in range(KC):
                    k0 = (j * KC + c) * P - n * XCOLS
                    last = nc.tensor.matmul(ps_z_v[j % len(ps_z)][:, c, :], raw[:, n, k0:k0 + P], wn_t,
                                            start=True, stop=True)
                last.then_inc(s_zp, 1)
            pe.wait_ge(s_const, 6 * 16)
            pe.wait_ge(s_fill, 1)
            nc.tensor.matmul(ps_mean[:, 0:F], averager[:, :], w1_sb[:, :], start=True, stop=True
                             ).then_inc(s_wmean, 1)

            def high(acc, n, w, first):
                for c in range(HALF):
                    for k, part in enumerate((w[1], w[0])):
                        nc.tensor.matmul(acc[:, :], part[:, c, :], a_hi[:, n, c, :],
                                         start=first and c + k == 0, stop=False)

            def low_part(acc, n, w, final):
                for c in range(HALF):
                    last = nc.tensor.matmul(acc[:, :], w[0][:, c, :], a_lo[:, n, c, :], start=False,
                                            stop=final and c == HALF - 1)
                return last

            def chunks(hi, lo, j, hh):
                return [t[:, j, hh * HALF:(hh + 1) * HALF, :] for t in (hi, lo)]

            def add_x(row):
                pe.wait_ge(s_w, 1)
                pe.wait_ge(s_xt, 16 * (row + 1))
                nc.tensor.matmul(acc2[:, :], ws_t[:, :], wide[:, :], start=False, stop=True
                                 ).then_inc(s_row, 1)

            def transpose_h(row):
                pe.wait_ge(s_ht, row + 1)
                pe.wait_ge(s_dinv, row + 1)
                for c in range(KC):
                    last = nc.tensor.transpose(ps_tr[:, c * P:(c + 1) * P], acc_t[:, c * P:(c + 1) * P],
                                               ident[:, :])
                last.then_inc(s_tr, 1)

            def project_h(row):
                for c in range(KC):
                    last = nc.tensor.matmul(ps_hw[:, c * F:(c + 1) * F], acc_t[:, c * P:(c + 1) * P],
                                            w1_sb[:, :], start=True, stop=True)
                last.then_inc(s_hw, 1)

            def layer0_steps(when, q, row):
                if q == when["turn"]:
                    transpose_h(row)
                    project_h(row)

            for s, lo, hi in ROWS1:
                with span(pe, lo, hi) as r:
                    row = SB * s + r
                    used = 2 * base1(s) + 2 * row_tiles(s) * r
                    if s + lo == 0:
                        pe.wait_ge(s_z, NB)
                    for k, u, q in row_halves(s):
                        n = k % RING
                        if u is not None:
                            bank = ps_late[u % 2]
                            g = chunks(g_hi, g_lo, SB * (s - 1) + q // 2, q % 2)
                            if u == 0 and q == 0:
                                pe.wait_ge(s_g, SB * s)
                            if q == 0 and SB * s + lo > SB:
                                pe.wait_ge(s_lowsum, late_rows(s) + r * s + max(u - 1, 0))
                            pe.wait_ge(s_hi, used + k + 1)
                            high(bank, n, g, q == 0)
                            pe.wait_ge(s_lo, used + k + 1)
                            low_part(bank, n, g, q == 2 * SB - 1).then_inc(s_used, 1)
                            continue
                        j = column(q)
                        bank = acc0 if q < FIRST else acc2
                        final = q == HALVES - 1
                        if q == 0 and s + lo > 0:
                            pe.wait_ge(s_oa, row)
                        if q == FIRST and s + lo > 0:
                            pe.wait_ge(s_ht, row)
                        z = chunks(z_hi, z_lo, j, q % 2)
                        pe.wait_ge(s_hi, used + k + 1)
                        high(bank, n, z, q % FIRST == 0)
                        pe.wait_ge(s_lo, used + k + 1)
                        last = low_part(bank, n, z, q == FIRST - 1)
                        if j < SB * s:
                            if final:
                                add_x(row)
                            g = chunks(g_hi, g_lo, j, q % 2)
                            if j == 0 and q % 2 == 0:
                                pe.wait_ge(s_g, SB * s - 1)
                                pe.wait_ge(s_lowown, row - SB)
                            if j == SB * s - 1 and q % 2 == 0:
                                pe.wait_ge(s_g, SB * s)
                            high(acc1, n, g, j == 0 and q % 2 == 0)
                            last = low_part(acc1, n, g, j == SB * s - 1 and q % 2 == 1)
                        last.then_inc(s_used, 1)
                        if final and j >= SB * s:
                            add_x(row)
                        if s + lo > 0:
                            layer0_steps(USUAL, q, row - 1)

            def transpose_ag(row):
                pe.wait_ge(s_relu, row + 1)
                for g in (g_lo, g_hi):
                    nc.tensor.matmul(ps_tr[:, :], ident_r[:, :],
                                     g[:, bass.ds(row, 1), :, :].rearrange("p o c f -> p (o c f)"),
                                     start=g is g_lo, stop=False)
                pe.wait_ge(s_ot, row + 1)
                for c in range(KC):
                    last = nc.tensor.matmul(ps_tr[:, c * P:(c + 1) * P], acc_t[:, c * P:(c + 1) * P],
                                            ident[:, :], start=False, stop=c == KC - 1)
                last.then_inc(s_tr, 1)

            pe.wait_ge(s_idr, 1)
            for lo, hi in PAIRS:
                first = lo == 0
                with span(pe, lo, hi) as pair:
                    for k, second, q in pair_halves(first):
                        row = pair * 2 + second
                        bank = acc1 if second else acc0
                        half = 2 * BASE2 + pair * 4 * SB + k
                        if q == 0 and not first:
                            pe.wait_ge(s_ot, row - 1)
                        elif q == 0 and second:
                            pe.wait_ge(s_lowown, NB - SB)
                        elif q == 0:
                            pe.wait_ge(s_oa, NB)
                        if first and not second and q == 2 * SB - 2:
                            pe.wait_ge(s_g, NB)
                        g = chunks(g_hi, g_lo, NB - SB + q // 2, q % 2)
                        pe.wait_ge(s_hi, half + 1)
                        high(bank, k % RING, g, q == 0)
                        pe.wait_ge(s_lo, half + 1)
                        low_part(bank, k % RING, g, q == 2 * SB - 1).then_inc(s_used, 1)
                        if first:
                            layer0_steps(EARLY, k, NB - 1)
                        for name, row in finish_steps(first, k, pair):
                            if name == "turn":
                                transpose_ag(row)
            transpose_ag(NB - 1)


def kernel(x, adj, L0_gnn_W, L0_gnn_b, L1_gnn_W, L1_gnn_b):
    import numpy as np
    import concourse.bacc as bacc
    from concourse.bass_utils import run_bass_kernel_spmd

    x, adj, w0, w1, b0, b1 = (np.asarray(a) for a in (x, adj, L0_gnn_W, L1_gnn_W, L0_gnn_b, L1_gnn_b))
    n, nb = x.shape[0], x.shape[0] // MB
    tiles = adj.reshape(nb, MB, nb, KC, P).transpose(0, 2, 4, 3, 1)
    tiles = np.roll(tiles, SB, axis=1)
    arrays = {
        "tiles": np.ascontiguousarray(tiles).reshape(nb * nb, P, KC * MB),
        "x_t": np.ascontiguousarray(x.T),
        "w0_t": np.ascontiguousarray(w0.T),
        "w1_t": np.ascontiguousarray(w1.T),
        "b0": np.ascontiguousarray(b0.reshape(F, 1)),
        "b1": np.ascontiguousarray(b1.reshape(1, F)),
        "eye": np.eye(P, dtype=np.float32),
    }
    nc = bacc.Bacc("TRN2", target_bir_lowering=False, num_devices=1)
    fp32 = mybir.dt.float32
    args = [nc.dram_tensor(name, a.shape, fp32, kind="ExternalInput").ap() for name, a in arrays.items()]
    out = nc.dram_tensor("out", (n, F), fp32, kind="ExternalOutput").ap()
    two_layers(nc, *args, out)
    result = run_bass_kernel_spmd(nc, [arrays], core_ids=[0])
    return result.results[0]["out"]
```
